# Optimizing a Trainium2 kernel written in Bass

```python
import numpy as np
import jax
import jax.numpy as jnp

def _softmax(x, axis=-1):
    return jax.nn.softmax(x, axis=axis)

def _gelu(x):
    return jax.nn.gelu(x, approximate=True)

def _silu(x):
    return jax.nn.silu(x)

def _sigmoid(x):
    return jax.nn.sigmoid(x)

def _layernorm(x, axis=-1, eps=1e-05):
    m = jnp.mean(x, axis=axis, keepdims=True)
    v = jnp.var(x, axis=axis, keepdims=True)
    return (x - m) / jnp.sqrt(v + eps)

def _scatter_add(tgt, idx, src, axis=0):
    return tgt.at[idx].add(src)

def _segment_sum(src, seg, n):
    return jax.ops.segment_sum(src, seg, n)
kernel_name = 'mk_vit_tower_cls_d1_tok_img1024_r4_d1e44b'

def setup_inputs(seed: int=0):
    np.random.seed(seed)
    _w = jnp.asarray

    def _rec_inputs():
        import jax
        import jax.numpy as jnp
        _rk = jax.random.key(seed)
        x = -0.00016672 + 0.999947 * jax.random.normal(jax.random.fold_in(_rk, 1), (16, 3, 96, 96), jnp.float32)
        cls_tok = 0.02 * jax.random.normal(jax.random.fold_in(_rk, 5), (1, 1, 256), jnp.float32)
        return (x, cls_tok)
    x, cls_tok = _rec_inputs()

    def _L0_tok_setup():
        import jax, jax.numpy as jnp
        import numpy as np
        B, C, H, W = (64, 3, 96, 96)
        P = 16
        HP, WP = (H // P, W // P)
        N = HP * WP
        F = C * P * P
        D = 256
        key = jax.random.key(seed)
        k1, k2, k3, k4, k5 = jax.random.split(key, 5)
        data = jax.random.normal(k1, (B, C, H, W), dtype=jnp.float32)
        lim = 1.0 / np.sqrt(F)
        W_lin = jax.random.uniform(k2, (D, F), minval=-lim, maxval=lim, dtype=jnp.float32)
        b_lin = jax.random.uniform(k3, (D,), minval=-lim, maxval=lim, dtype=jnp.float32)
        class_token = jax.random.normal(k4, (1, 1, D), dtype=jnp.float32)
        position_embeddings = jax.random.normal(k5, (1, N + 1, D), dtype=jnp.float32)
        return {'data': data, 'W_lin': W_lin, 'b_lin': b_lin, 'class_token': class_token, 'position_embeddings': position_embeddings}
    _L0_tok_all = _L0_tok_setup()
    _L0_tok_in = {k: v for k, v in _L0_tok_all.items() if k in ('W_lin', 'b_lin', 'class_token', 'position_embeddings')}
    del _L0_tok_all

    def _L0_attn_setup():
        import jax, jax.numpy as jnp
        import numpy as np
        D_IN, HEAD_DIM = (256, 128)
        key = jax.random.key(seed)
        ks = jax.random.split(key, 9)
        s = 0.02
        return {'x': jax.random.normal(ks[0], (4, 1024, D_IN), dtype=jnp.float32), 'Wq': jax.random.normal(ks[1], (HEAD_DIM, D_IN), dtype=jnp.float32) * s, 'bq': jnp.zeros((HEAD_DIM,), dtype=jnp.float32), 'Wk': jax.random.normal(ks[2], (HEAD_DIM, D_IN), dtype=jnp.float32) * s, 'bk': jnp.zeros((HEAD_DIM,), dtype=jnp.float32), 'Wv': jax.random.normal(ks[3], (HEAD_DIM, D_IN), dtype=jnp.float32) * s, 'bv': jnp.zeros((HEAD_DIM,), dtype=jnp.float32), 'Wo': jax.random.normal(ks[4], (D_IN, HEAD_DIM), dtype=jnp.float32) * s, 'bo': jnp.zeros((D_IN,), dtype=jnp.float32)}
    _L0_attn_all = _L0_attn_setup()
    _L0_attn_in = {k: v for k, v in _L0_attn_all.items() if k in ('Wq', 'bq', 'Wk', 'bk', 'Wv', 'bv', 'Wo', 'bo')}
    del _L0_attn_all

    def _L0_ffn_setup():
        import jax, jax.numpy as jnp
        import numpy as np
        THRESHOLD = 0.1
        key = jax.random.key(seed)
        k1, k2, k3 = jax.random.split(key, 3)
        B, S, D, E = (4, 1024, 256, 8)
        inputs = jax.random.normal(k1, (B, S, D), dtype=jnp.float32)
        gate_w = jax.random.normal(k2, (D, E), dtype=jnp.float32) * 0.02
        gate_b = jnp.zeros((E,), dtype=jnp.float32)
        expert_w = jax.random.normal(k3, (E, D, D), dtype=jnp.float32) * 0.02
        expert_b = jnp.zeros((E, D), dtype=jnp.float32)
        return {'inputs': inputs, 'gate_w': gate_w, 'gate_b': gate_b, 'expert_w': expert_w, 'expert_b': expert_b}
    _L0_ffn_all = _L0_ffn_setup()
    _L0_ffn_in = {k: v for k, v in _L0_ffn_all.items() if k in ('gate_w', 'gate_b', 'expert_w', 'expert_b')}
    del _L0_ffn_all
    return {'x': x, 'cls_tok': cls_tok, 'L0_tok_W_lin': _L0_tok_in['W_lin'], 'L0_tok_b_lin': _L0_tok_in['b_lin'], 'L0_tok_class_token': _L0_tok_in['class_token'], 'L0_tok_position_embeddings': _L0_tok_in['position_embeddings'], 'L0_attn_Wq': _L0_attn_in['Wq'], 'L0_attn_bq': _L0_attn_in['bq'], 'L0_attn_Wk': _L0_attn_in['Wk'], 'L0_attn_bk': _L0_attn_in['bk'], 'L0_attn_Wv': _L0_attn_in['Wv'], 'L0_attn_bv': _L0_attn_in['bv'], 'L0_attn_Wo': _L0_attn_in['Wo'], 'L0_attn_bo': _L0_attn_in['bo'], 'L0_ffn_gate_w': _L0_ffn_in['gate_w'], 'L0_ffn_gate_b': _L0_ffn_in['gate_b'], 'L0_ffn_expert_w': _L0_ffn_in['expert_w'], 'L0_ffn_expert_b': _L0_ffn_in['expert_b']}

def reference(x, cls_tok, L0_tok_W_lin, L0_tok_b_lin, L0_tok_class_token, L0_tok_position_embeddings, L0_attn_Wq, L0_attn_bq, L0_attn_Wk, L0_attn_bk, L0_attn_Wv, L0_attn_bv, L0_attn_Wo, L0_attn_bo, L0_ffn_gate_w, L0_ffn_gate_b, L0_ffn_expert_w, L0_ffn_expert_b):
    import jax
    import jax.numpy as jnp

    def _L0_tok_ref(data, W_lin, b_lin, class_token, position_embeddings):
        import jax, jax.numpy as jnp
        import numpy as np
        B, C, H, W = (64, 3, 96, 96)
        P = 16
        HP, WP = (H // P, W // P)
        N = HP * WP
        F = C * P * P
        D = 256
        b = data.shape[0]
        x = data.reshape(b, C, HP, P, WP, P)
        x = x.transpose(0, 2, 4, 1, 3, 5).reshape(b, N, F)
        x = jnp.einsum('bnf,df->bnd', x, W_lin) + b_lin
        cls = jnp.broadcast_to(class_token, (b, 1, D))
        out = jnp.concatenate([cls, x], axis=1) + position_embeddings
        return out

    def _L0_attn_ref(x, Wq, bq, Wk, bk, Wv, bv, Wo, bo):
        import jax, jax.numpy as jnp
        import numpy as np
        D_IN, HEAD_DIM = (256, 128)
        B, S, D = x.shape
        Q = jnp.einsum('bsd,hd->bsh', x, Wq) + bq
        K = jnp.einsum('bsd,hd->bsh', x, Wk) + bk
        V = jnp.einsum('bsd,hd->bsh', x, Wv) + bv
        scores = jnp.einsum('bqh,bkh->bqk', Q, K)
        causal = jnp.tril(jnp.ones((S, S), dtype=bool))
        scores = jnp.where(causal, scores, -jnp.inf)
        scale = jnp.float32(HEAD_DIM) ** (-0.5)
        attn = jax.nn.softmax(scores * scale, axis=-1)
        out = jnp.einsum('bqk,bkh->bqh', attn, V)
        return jnp.einsum('bsh,dh->bsd', out, Wo) + bo

    def _L0_ffn_ref(inputs, gate_w, gate_b, expert_w, expert_b):
        import jax, jax.numpy as jnp
        import numpy as np
        THRESHOLD = 0.1
        d = inputs.shape[-1]
        x = inputs.reshape(-1, d)
        gate_logits = jax.nn.softmax(x @ gate_w + gate_b, axis=-1)
        selected = (gate_logits >= THRESHOLD).astype(x.dtype)
        weights = gate_logits * selected
        wsum = jnp.sum(weights, axis=-1, keepdims=True)
        weights = weights / jnp.where(wsum == 0, jnp.ones_like(wsum), wsum)
        E = expert_w.shape[0]
        out = jnp.zeros((x.shape[0], expert_w.shape[-1]), dtype=x.dtype)
        for e in range(E):
            out = out + weights[:, e:e + 1] * (x @ expert_w[e] + expert_b[e])
        return out.reshape(*inputs.shape[:-1], out.shape[-1])
    h = _L0_tok_ref(x, L0_tok_W_lin, L0_tok_b_lin, L0_tok_class_token, L0_tok_position_embeddings)
    h = jnp.concatenate([jnp.broadcast_to(cls_tok, (h.shape[0], 1, h.shape[2])), h], axis=1)
    h = h + _L0_attn_ref(_layernorm(h, axis=-1), L0_attn_Wq, L0_attn_bq, L0_attn_Wk, L0_attn_bk, L0_attn_Wv, L0_attn_bv, L0_attn_Wo, L0_attn_bo)
    h = h + _L0_ffn_ref(_layernorm(h, axis=-1), L0_ffn_gate_w, L0_ffn_gate_b, L0_ffn_expert_w, L0_ffn_expert_b)
    return h

_drawn_inputs = setup_inputs


def setup_inputs(seed=0):
    import zlib

    import numpy as np

    out = dict(_drawn_inputs(seed))
    spreads = {'L0_attn_bq': (0.0, 0.8),
     'L0_attn_bk': (0.0, 0.8),
     'L0_attn_bv': (0.0, 0.419),
     'L0_attn_bo': (0.0, 0.1),
     'L0_ffn_gate_b': (0.0, 0.1),
     'L0_ffn_expert_b': (0.0, 0.1)}
    factors = {'cls_tok': 3.126, 'L0_tok_b_lin': 2.949, 'L0_attn_Wq': 8.0, 'L0_attn_Wk': 8.0}
    for name, (base, spread) in spreads.items():
        noise = np.random.default_rng([zlib.crc32(name.encode()), seed]).standard_normal(out[name].shape)
        drawn = base * np.exp(spread * noise) if base else spread * noise
        out[name] = jnp.asarray(drawn.astype(out[name].dtype))
    for name, factor in factors.items():
        out[name] = (out[name] * factor).astype(out[name].dtype)
    return out
```

```python
from contextlib import ExitStack

import concourse.bass as bass
from concourse import mybir

F32 = mybir.dt.float32
F32R = mybir.dt.float32r
ALU = mybir.AluOpType
ACT = mybir.ActivationFunctionType

P = 128
IMAGES, CHANNELS, SIDE, PATCH = 16, 3, 96, 16
GRID = SIDE // PATCH
SEQ = GRID * GRID + 2
TOKENS = IMAGES * SEQ
D = 256
DC = D // P
F = CHANNELS * PATCH * PATCH
FC = F // P
HEAD = 128
EXPERTS = 8
THRESHOLD = 0.1
EPS = 1e-5
TILES = -(-TOKENS // P)
IMAGES_PER_GROUP = P // SEQ
GROUP = IMAGES_PER_GROUP * SEQ
GROUPS = -(-TOKENS // GROUP)
BANK = 512
QUARTERS = EXPERTS * D // BANK
PER_QUARTER = EXPERTS // QUARTERS
H_BANKS, Y_BANKS = 3, 3
CLOSED = -1.0e30

TABLE_LO = 64
TABLE_ROWS = TABLE_LO + SEQ
BO_ROWS = 33
EB_ROWS = 64 + EXPERTS

TILE = [(P * t, min(P, TOKENS - P * t)) for t in range(TILES)]
SPAN = [(GROUP * g, min(GROUP, TOKENS - GROUP * g)) for g in range(GROUPS)]

def _columns():
    at, n = {}, 0
    for name, width in (("table_a", D), ("table_b", D), ("onehot", TOKENS), ("ident", P),
                        ("wqkv", DC * 3 * HEAD), ("biases", 3), ("mask", GROUP), ("wo", D), ("bo", D),
                        ("gate_w", DC * EXPERTS), ("gate_b", EXPERTS), ("expert_b", D)):
        at[name] = (n, n + width)
        n += width
    return at, n


COL, SMALL = _columns()
FIRST_SMALL = COL["ident"][0]


def _schedule():
    groups_of = [[g for g in range(GROUPS) if (SPAN[g][0] + SPAN[g][1] - 1) // P == t] for t in range(TILES)]

    def attention_scores(t):
        return [("T1", t), ("QK", t)] + [("VS", g) for g in groups_of[t]]

    def attention_values(t):
        return [(s, g) for g in groups_of[t] for s in ("P", "PT", "OT")]

    s = [("E", 0), ("E", 1), ("N1", 0), ("E", 2)] + attention_scores(0) + [("N1", 1)] + attention_scores(1)
    s += attention_values(0) + attention_values(1) + [("N1", 2), ("O", 0)] + attention_scores(2)
    s += [("N2", 0), ("T2", 0)] + attention_values(2) + [("O", 1), ("G", 0), ("N2", 1), ("W", 0)]
    for t in range(TILES):
        s += [("B", t), (("Y", 0), t)]
        if t + 3 < TILES:
            s += [("E", t + 3)]
        if t + 1 < TILES:
            s += [("T2", t + 1)]
        s += [(("Y", 1), t)]
        if t + 1 < TILES:
            s += [("G", t + 1)]
        if t + 3 < TILES:
            s += [("N1", t + 3), ("T1", t + 3), ("QK", t + 3)]
        s += [(("Y", 2), t)]
        if t + 1 < TILES:
            s += [("W", t + 1)]
        if t + 3 < TILES:
            s += [("VS", g) for g in groups_of[t + 3]]
        s += [(("Y", 3), t)]
        if t + 3 < TILES:
            s += attention_values(t + 3)
        if t + 2 < TILES:
            s += [("O", t + 2), ("N2", t + 2)]
    return s


SCHEDULE = _schedule()
DVE_X_TILES = 2
DVE_QUARTERS = 2


def build(nc, x_t, w_lin_t, small, expert_w, out):
    ctx = ExitStack()
    with ctx:
        def sb(name, shape, dt=F32):
            return ctx.enter_context(nc.sbuf_tensor(name, shape, dt))

        def psum(name):
            return ctx.enter_context(nc.psum_tensor(name, [P, BANK], F32))

        def sem(name):
            return ctx.enter_context(nc.semaphore(name))

        x_raw = sb("x_raw", [P, FC * TOKENS])
        x_hi = sb("x_hi", [P, FC * TOKENS], F32R)
        x_lo = sb("x_lo", [P, FC * TOKENS], F32R)
        wl_raw = sb("wl_raw", [P, FC, D])
        wl_hi = sb("wl_hi", [P, FC, D], F32R)
        wl_lo = sb("wl_lo", [P, FC, D], F32R)
        ew_raw = sb("ew_raw", [P, QUARTERS, DC, BANK])
        ew_hi = sb("ew_hi", [P, QUARTERS, DC, BANK], F32R)
        ew_lo = sb("ew_lo", [P, QUARTERS, DC, BANK], F32R)
        sm = sb("sm", [P, SMALL])
        table_sum = sb("table_sum", [P, D])
        table = sb("table", [P, D], F32R)
        onehot = sb("onehot", [P, TOKENS], F32R)
        ones = sb("ones", [P, P], F32R)
        bo = sb("bo", [P, D], F32R)
        eb = sb("eb", [P, D], F32R)
        stats = sb("stats", [P, 2, TILES, 6])
        moments = sb("moments", [P, 2, TILES, 2])
        var_eps = sb("var_eps", [P, 2, TILES, 1])
        minus_half = sb("minus_half", [P, 1])
        rstd = sb("rstd", [P, 2, TILES, 1])
        xn1 = sb("xn1", [P, TILES, D])
        xn1_t = sb("xn1_t", [P, DC, TOKENS])
        q_t = sb("q_t", [P, TOKENS])
        k_t = sb("k_t", [P, TOKENS])
        v = sb("v", [P, GROUPS, HEAD])
        scores = sb("scores", [P, GROUPS, GROUP])
        row_max = sb("row_max", [P, GROUPS])
        exp_bias = sb("exp_bias", [P, GROUPS])
        row_sum = sb("row_sum", [P, GROUPS])
        row_inv = sb("row_inv", [P, GROUPS])
        probs = sb("probs", [P, GROUPS, GROUP])
        probs_n = sb("probs_n", [P, GROUPS, GROUP])
        probs_t = sb("probs_t", [P, GROUPS, GROUP])
        o_t = sb("o_t", [P, TOKENS])
        xn2 = sb("xn2", [P, TILES, D])
        xn2_t = sb("xn2_t", [P, TILES, DC, P])
        xn2_hi = sb("xn2_hi", [P, TILES, DC, P], F32R)
        xn2_lo = sb("xn2_lo", [P, TILES, DC, P], F32R)
        logits = sb("logits", [P, TILES, EXPERTS])
        gates = sb("gates", [P, TILES, EXPERTS])
        picked = sb("picked", [P, TILES, EXPERTS])
        weights = sb("weights", [P, TILES, EXPERTS])
        gate_cols = sb("gate_cols", [P, TILES, 8])
        w_stack = sb("w_stack", [P, TILES, EB_ROWS], F32R)
        w_stack_t = sb("w_stack_t", [P, TILES, P], F32R)
        acc = sb("acc", [P, TILES, D])

        h_bank = [psum(f"h_bank{i}") for i in range(H_BANKS)]
        y_bank = [psum(f"y_bank{i}") for i in range(Y_BANKS)]
        turn_bank = psum("turn_bank")
        mix_bank = psum("mix_bank")

        def col(name, rows=P):
            return sm[0:rows, COL[name][0]:COL[name][1]]

        ident = col("ident")
        wqkv = col("wqkv").rearrange("p (c m h) -> p c m h", c=DC, m=3)
        gate_w = col("gate_w").rearrange("p (c e) -> p c e", c=DC)

        def x_of(buf, t):
            t0, n = TILE[t]
            return buf[:, FC * t0:FC * (t0 + n)]

        wl_in = [sem(f"wl_in{i}") for i in range(3)]
        x_in = [sem(f"x_in{t}") for t in range(TILES)]
        table_in, small_in = sem("table_in"), sem("small_in")
        ew_in = [sem(f"ew_in{q}") for q in range(QUARTERS)]
        out_stored = sem("out_stored")
        wl_hi_ready, wl_lo_ready = sem("wl_hi_ready"), sem("wl_lo_ready")
        x_hi_ready, x_lo_dve, x_lo_pool = sem("x_hi_ready"), sem("x_lo_dve"), sem("x_lo_pool")
        table_ready, onehot_ready, ones_ready = sem("table_ready"), sem("onehot_ready"), sem("ones_ready")
        bias_tables_ready, stack_cleared, half_ready = sem("bias_tables_ready"), sem("stack_cleared"), sem("half_ready")
        ew_hi_ready, ew_lo_dve, ew_lo_pool = sem("ew_hi_ready"), sem("ew_lo_dve"), sem("ew_lo_pool")
        dve_step = sem("dve_step")
        embedded, projected = sem("embedded"), sem("projected")
        var_ready, rstd_ready = [sem("var1_ready"), sem("var2_ready")], [sem("rstd1_ready"), sem("rstd2_ready")]
        xn1_ready, xn2_ready = sem("xn1_ready"), sem("xn2_ready")
        xn1_turned, xn1_t_ready = sem("xn1_turned"), sem("xn1_t_ready")
        qk_done, qk_ready = sem("qk_done"), sem("qk_ready")
        vs_done, v_ready, s_ready = sem("vs_done"), sem("v_ready"), sem("s_ready")
        exp_bias_ready, probs_ready, probs_n_ready = sem("exp_bias_ready"), sem("probs_ready"), sem("probs_n_ready")
        probs_turned, probs_t_ready = sem("probs_turned"), sem("probs_t_ready")
        o_done, o_t_ready = sem("o_done"), sem("o_t_ready")
        xn2_turned, xn2_t_ready = sem("xn2_turned"), sem("xn2_t_ready")
        xn2_hi_ready, xn2_lo_ready = sem("xn2_hi_ready"), sem("xn2_lo_ready")
        gate_done, logits_ready, gate_max_ready, gate_exp_ready = sem("gate_done"), sem("logits_ready"), sem("gate_max_ready"), sem("gate_exp_ready")
        weights_ready, weights_turned, w_stack_t_ready = sem("weights_ready"), sem("weights_turned"), sem("w_stack_t_ready")
        biased, acc_ready = sem("biased"), sem("acc_ready")
        y_done, y_used, out_ready = sem("y_done"), sem("y_used"), sem("out_ready")

        block = ctx.enter_context(nc.Block())

        @block.sync
        def _(sp):
            def load_x(t):
                sp.dma_start(x_of(x_raw, t), x_of(x_t, t)).then_inc(x_in[t], 16)

            def load_ew(q):
                sp.dma_start(ew_raw[:, q, :, :], expert_w[:, q, :, :]).then_inc(ew_in[q], 16)

            sp.dma_start(wl_raw[:, 0:2, :], w_lin_t[:, 0:2, :]).then_inc(wl_in[0], 16)
            load_x(0)
            sp.dma_start(wl_raw[:, 2:4, :], w_lin_t[:, 2:4, :]).then_inc(wl_in[1], 16)
            sp.dma_start(wl_raw[:, 4:6, :], w_lin_t[:, 4:6, :]).then_inc(wl_in[2], 16)
            sp.dma_start(sm[:, 0:FIRST_SMALL], small[:, 0:FIRST_SMALL]).then_inc(table_in, 16)
            load_x(1)
            sp.dma_start(sm[:, FIRST_SMALL:], small[:, FIRST_SMALL:]).then_inc(small_in, 16)
            load_x(2)
            load_ew(0)
            load_ew(1)
            load_x(3)
            load_ew(2)
            load_ew(3)
            load_x(4)
            for t in range(TILES):
                t0, n = TILE[t]
                sp.wait_ge(out_ready, t + 1)
                sp.dma_start(out[t0:t0 + n, :], acc[0:n, t, :]).then_inc(out_stored, 16)
            sp.wait_ge(out_stored, 16 * TILES)

        @block.gpsimd
        def _(pool):
            nc.gpsimd.memset(minus_half[:], -0.5).then_inc(half_ready, 1)
            pool.wait_ge(half_ready, 1)
            pool_x = list(range(DVE_X_TILES, TILES))
            pool_q = list(range(DVE_QUARTERS, QUARTERS))

            def x_low(t):
                pool.wait_ge(x_hi_ready, t + 1)
                nc.gpsimd.tensor_tensor(x_of(x_lo, t), x_of(x_raw, t), x_of(x_hi, t).bitcast(F32),
                                        ALU.subtract).then_inc(x_lo_pool, 1)

            def ew_low(q):
                pool.wait_ge(ew_hi_ready, q + 1)
                for c in range(DC):
                    nc.gpsimd.tensor_tensor(ew_lo[:, q, c, :], ew_raw[:, q, c, :], ew_hi[:, q, c, :].bitcast(F32),
                                            ALU.subtract).then_inc(ew_lo_pool, 1)

            def power(which, t):
                n = TILE[t][1]
                pool.wait_ge(var_ready[which], t + 1)
                nc.gpsimd.tensor_tensor(rstd[0:n, which, t, :], var_eps[0:n, which, t, :], minus_half[0:n, :],
                                        ALU.pow).then_inc(rstd_ready[which], 1)

            for stage, t in SCHEDULE:
                if stage == "E":
                    power(0, t)
                    if pool_x:
                        x_low(pool_x.pop(0))
                if stage == "VS" and pool_q:
                    ew_low(pool_q.pop(0))
                if stage == "O":
                    power(1, t)

        @block.scalar
        def _(act):
            def x_high(t):
                act.wait_ge(x_in[t], 16)
                nc.scalar.copy(x_of(x_hi, t), x_of(x_raw, t)).then_inc(x_hi_ready, 1)

            def ew_high(q):
                act.wait_ge(ew_in[q], 16)
                nc.scalar.copy(ew_hi[:, q, :, :], ew_raw[:, q, :, :]).then_inc(ew_hi_ready, 1)

            def wl_high(i):
                act.wait_ge(wl_in[i], 16)
                nc.scalar.copy(wl_hi[:, 2 * i:2 * i + 2, :], wl_raw[:, 2 * i:2 * i + 2, :]).then_inc(wl_hi_ready, 1)

            wl_high(0)
            x_high(0)
            wl_high(1)
            wl_high(2)
            act.wait_ge(table_in, 16)
            nc.scalar.copy(onehot[0:TABLE_ROWS, :], col("onehot", TABLE_ROWS)).then_inc(onehot_ready, 1)
            x_high(1)
            x_high(2)
            act.wait_ge(small_in, 16)
            later = [lambda: ew_high(0), lambda: ew_high(1), lambda: x_high(3), lambda: ew_high(2),
                     lambda: ew_high(3), lambda: x_high(4)]

            for stage, t in SCHEDULE:
                if stage in ("VS", "T1", "QK") and t <= 2 and later:
                    pass
                if stage == "T1":
                    t0, n = TILE[t]
                    act.wait_ge(xn1_turned, t + 1)
                    nc.scalar.copy(xn1_t[:, :, t0:t0 + n],
                                   turn_bank[:, 0:DC * P].rearrange("p (c n) -> p c n", c=DC)[:, :, 0:n]
                                   ).then_inc(xn1_t_ready, 1)
                elif stage == "QK":
                    t0, n = TILE[t]
                    act.wait_ge(qk_done, t + 1)
                    nc.scalar.activation(q_t[:, t0:t0 + n], mix_bank[:, 0:n], ACT.Identity,
                                         bias=col("biases")[:, 0:1]).then_inc(qk_ready, 1)
                    nc.scalar.activation(k_t[:, t0:t0 + n], mix_bank[:, P:P + n], ACT.Identity,
                                         bias=col("biases")[:, 1:2]).then_inc(qk_ready, 1)
                elif stage == "VS":
                    n = SPAN[t][1]
                    act.wait_ge(exp_bias_ready, t + 1)
                    nc.scalar.activation(probs[0:n, t, 0:n], scores[0:n, t, 0:n], ACT.Exp,
                                         bias=exp_bias[0:n, t:t + 1], scale=float(HEAD) ** -0.5,
                                         accum_out=row_sum[0:n, t:t + 1]).then_inc(probs_ready, 1)
                    if later:
                        later.pop(0)()
                        later.pop(0)()
                elif stage == "PT":
                    n = SPAN[t][1]
                    act.wait_ge(probs_turned, t + 1)
                    nc.scalar.copy(probs_t[0:n, t, 0:n], turn_bank[0:n, 0:n]).then_inc(probs_t_ready, 1)
                elif stage == "OT":
                    t0, n = SPAN[t]
                    act.wait_ge(o_done, t + 1)
                    nc.scalar.activation(o_t[:, t0:t0 + n], mix_bank[:, 0:n], ACT.Identity,
                                         bias=col("biases")[:, 2:3]).then_inc(o_t_ready, 1)
                elif stage == "T2":
                    n = TILE[t][1]
                    act.wait_ge(xn2_turned, t + 1)
                    src = turn_bank[:, 0:DC * P].rearrange("p (c n) -> p c n", c=DC)[:, :, 0:n]
                    nc.scalar.copy(xn2_hi[:, t, :, 0:n], src).then_inc(xn2_hi_ready, 1)
                    nc.scalar.copy(xn2_t[:, t, :, 0:n], src).then_inc(xn2_t_ready, 1)
                elif stage == "G":
                    n = TILE[t][1]
                    act.wait_ge(gate_max_ready, t + 1)
                    nc.scalar.activation(gates[0:n, t, :], logits[0:n, t, :], ACT.Exp,
                                         bias=gate_cols[0:n, t, 1:2],
                                         accum_out=gate_cols[0:n, t, 2:3]).then_inc(gate_exp_ready, 1)
                elif stage == "B":
                    n = TILE[t][1]
                    act.wait_ge(weights_turned, t + 1)
                    nc.scalar.copy(w_stack_t[0:EB_ROWS, t, 0:n], turn_bank[0:EB_ROWS, 0:n]).then_inc(w_stack_t_ready, 1)
                    act.wait_ge(biased, t + 1)
                    nc.scalar.copy(acc[0:n, t, :], h_bank[t % H_BANKS][0:n, 0:D]).then_inc(acc_ready, 1)

        @block.vector
        def _(dve):
            steps = [0]

            def then(ins):
                steps[0] += 1
                ins.then_inc(dve_step, 1)
                dve.wait_ge(dve_step, steps[0])

            def low(out_ap, raw, hi):
                return nc.vector.tensor_tensor(out_ap, raw, hi.bitcast(F32), ALU.subtract)

            def wl_low(i):
                dve.wait_ge(wl_hi_ready, i + 1)
                s = slice(2 * i, 2 * i + 2)
                low(wl_lo[:, s, :], wl_raw[:, s, :], wl_hi[:, s, :]).then_inc(wl_lo_ready, 1)

            def x_low(t):
                dve.wait_ge(x_hi_ready, t + 1)
                low(x_of(x_lo, t), x_of(x_raw, t), x_of(x_hi, t)).then_inc(x_lo_dve, 1)

            def norm_stats(which, t, bank):
                n = TILE[t][1]
                then(nc.vector.bn_stats(stats[0:n, which, t, :], bank[0:n, 0:D]))
                then(nc.vector.bn_aggr(moments[0:n, which, t, :], stats[0:n, which, t, :]))
                nc.vector.tensor_scalar_add(var_eps[0:n, which, t, :], moments[0:n, which, t, 1:2],
                                            EPS).then_inc(var_ready[which], 1)

            def normalise(which, t, out_ap, bank):
                n = TILE[t][1]
                dve.wait_ge(rstd_ready[which], t + 1)
                return nc.vector.tensor_scalar(out_ap, bank[0:n, 0:D], moments[0:n, which, t, 0:1],
                                               rstd[0:n, which, t, :], ALU.subtract, ALU.mult)

            nc.vector.memset(ones[:].bitcast(F32), 1.0).then_inc(ones_ready, 1)
            nc.vector.memset(w_stack[:].bitcast(F32), 0.0).then_inc(stack_cleared, 1)
            wl_low(0)
            x_low(0)
            wl_low(1)
            wl_low(2)
            dve.wait_ge(table_in, 16)
            rows = slice(0, TABLE_ROWS)
            then(nc.vector.tensor_tensor(table_sum[rows, :], col("table_a", TABLE_ROWS), col("table_b", TABLE_ROWS),
                                         ALU.add))
            then(nc.vector.tensor_copy(table[rows, :], table_sum[rows, :]))
            rows = slice(TABLE_LO, TABLE_ROWS)
            low(table[rows, :], table_sum[rows, :], table[rows, :]).then_inc(table_ready, 1)
            x_low(1)
            dve.wait_ge(small_in, 16)
            then(nc.vector.tensor_copy(bo[0:BO_ROWS, :], col("bo", BO_ROWS)))
            low(bo[32:33, :], sm[32:33, COL["bo"][0]:COL["bo"][1]], bo[32:33, :]).then_inc(bias_tables_ready, 1)
            then(nc.vector.tensor_copy(eb[0:EB_ROWS, :], col("expert_b", EB_ROWS)))
            rows = slice(32, 32 + EXPERTS)
            low(eb[rows, :], sm[rows, COL["expert_b"][0]:COL["expert_b"][1]], eb[rows, :]).then_inc(bias_tables_ready, 1)
            dve_q = list(range(DVE_QUARTERS))

            for stage, t in SCHEDULE:
                if stage == "E":
                    dve.wait_ge(embedded, t + 1)
                    norm_stats(0, t, h_bank[t % H_BANKS])
                elif stage == "N1":
                    n = TILE[t][1]
                    normalise(0, t, xn1[0:n, t, :], h_bank[t % H_BANKS]).then_inc(xn1_ready, 1)
                elif stage == "VS":
                    n = SPAN[t][1]
                    dve.wait_ge(vs_done, t + 1)
                    nc.vector.tensor_tensor_reduce(out=scores[0:n, t, 0:n], in0=mix_bank[0:n, HEAD:HEAD + n],
                                                   in1=col("mask")[0:n, 0:n], scale=1.0, scalar=-3.0e38,
                                                   op0=ALU.add, op1=ALU.max,
                                                   accum_out=row_max[0:n, t:t + 1]).then_inc(s_ready, 1)
                    nc.vector.tensor_copy(v[0:n, t, :], mix_bank[0:n, 0:HEAD]).then_inc(v_ready, 1)
                    dve.wait_ge(s_ready, t + 1)
                    nc.vector.tensor_scalar(exp_bias[0:n, t:t + 1], row_max[0:n, t:t + 1],
                                            -float(HEAD) ** -0.5, None, ALU.mult).then_inc(exp_bias_ready, 1)
                    if dve_q:
                        q = dve_q.pop(0)
                        dve.wait_ge(ew_hi_ready, q + 1)
                        low(ew_lo[:, q, :, :], ew_raw[:, q, :, :], ew_hi[:, q, :, :]).then_inc(ew_lo_dve, 1)
                elif stage == "P":
                    n = SPAN[t][1]
                    dve.wait_ge(probs_ready, t + 1)
                    then(nc.vector.reciprocal(row_inv[0:n, t:t + 1], row_sum[0:n, t:t + 1]))
                    nc.vector.tensor_scalar(probs_n[0:n, t, 0:n], probs[0:n, t, 0:n], row_inv[0:n, t:t + 1], None,
                                            ALU.mult).then_inc(probs_n_ready, 1)
                elif stage == "O":
                    dve.wait_ge(projected, t + 1)
                    norm_stats(1, t, h_bank[t % H_BANKS])
                elif stage == "N2":
                    n = TILE[t][1]
                    normalise(1, t, xn2[0:n, t, :], h_bank[t % H_BANKS]).then_inc(xn2_ready, 1)
                elif stage == "T2":
                    n = TILE[t][1]
                    dve.wait_ge(xn2_t_ready, t + 1)
                    low(xn2_lo[:, t, :, 0:n], xn2_t[:, t, :, 0:n], xn2_hi[:, t, :, 0:n]).then_inc(xn2_lo_ready, 1)
                elif stage == "G":
                    n = TILE[t][1]
                    dve.wait_ge(gate_done, t + 1)
                    nc.vector.tensor_tensor_reduce(out=logits[0:n, t, :], in0=mix_bank[0:n, 0:EXPERTS],
                                                   in1=col("gate_b")[0:n, :], scale=1.0, scalar=-3.0e38,
                                                   op0=ALU.add, op1=ALU.max,
                                                   accum_out=gate_cols[0:n, t, 0:1]).then_inc(logits_ready, 1)
                    dve.wait_ge(logits_ready, t + 1)
                    nc.vector.tensor_scalar(gate_cols[0:n, t, 1:2], gate_cols[0:n, t, 0:1], -1.0, None,
                                            ALU.mult).then_inc(gate_max_ready, 1)
                elif stage == "W":
                    n = TILE[t][1]
                    c = gate_cols[0:n, t, :]
                    dve.wait_ge(gate_exp_ready, t + 1)
                    then(nc.vector.reciprocal(c[:, 3:4], c[:, 2:3]))
                    then(nc.vector.tensor_scalar(gates[0:n, t, :], gates[0:n, t, :], c[:, 3:4], None, ALU.mult))
                    then(nc.vector.scalar_tensor_tensor(out=picked[0:n, t, :], in0=gates[0:n, t, :], scalar=THRESHOLD,
                                                        in1=gates[0:n, t, :], op0=ALU.is_ge, op1=ALU.mult,
                                                        accum_out=c[:, 4:5]))
                    then(nc.vector.scalar_tensor_tensor(out=c[:, 5:6], in0=c[:, 4:5], scalar=0.0, in1=c[:, 4:5],
                                                        op0=ALU.is_equal, op1=ALU.add))
                    then(nc.vector.reciprocal(c[:, 6:7], c[:, 5:6]))
                    then(nc.vector.tensor_scalar(weights[0:n, t, :], picked[0:n, t, :], c[:, 6:7], None, ALU.mult))
                    if t == 0:
                        dve.wait_ge(stack_cleared, 1)
                    then(nc.vector.tensor_copy(w_stack[0:n, t, 0:EXPERTS], weights[0:n, t, :]))
                    nc.vector.tensor_copy(w_stack[0:n, t, 32:32 + EXPERTS], weights[0:n, t, :]).then_inc(weights_ready, 1)
                    low(w_stack[0:n, t, 64:64 + EXPERTS], weights[0:n, t, :],
                        w_stack[0:n, t, 0:EXPERTS]).then_inc(weights_ready, 1)
                elif stage[0] == "Y":
                    n, q = TILE[t][1], stage[1]
                    i = QUARTERS * t + q
                    if q == 0:
                        dve.wait_ge(acc_ready, t + 1)
                    dve.wait_ge(y_done, i + 1)
                    for j in range(PER_QUARTER):
                        e = PER_QUARTER * q + j
                        ins = nc.vector.scalar_tensor_tensor(
                            out=acc[0:n, t, :], in0=y_bank[i % Y_BANKS][0:n, j * D:(j + 1) * D],
                            scalar=weights[0:n, t, e:e + 1], in1=acc[0:n, t, :], op0=ALU.mult, op1=ALU.add)
                        if j < PER_QUARTER - 1:
                            then(ins)
                        elif q < QUARTERS - 1:
                            ins.then_inc(y_used, 1)
                            dve.wait_ge(y_used, i + 1 - t)
                        else:
                            ins.then_inc(out_ready, 1)

        @block.tensor
        def _(pe):
            def three(out_ap, stat_hi, stat_lo, mov_hi, mov_lo, start, stop):
                nc.tensor.matmul(out_ap, stat_hi, mov_hi, start=start, stop=False, skip_group_check=True)
                nc.tensor.matmul(out_ap, stat_hi, mov_lo, start=False, stop=False, skip_group_check=True)
                return nc.tensor.matmul(out_ap, stat_lo, mov_hi, start=False, stop=stop, skip_group_check=True)

            for stage, t in SCHEDULE:
                if stage == "E":
                    t0, n = TILE[t]
                    h = h_bank[t % H_BANKS][0:n, 0:D]
                    if t >= H_BANKS:
                        pe.wait_ge(acc_ready, t - H_BANKS + 1)
                    if t < DVE_X_TILES:
                        pe.wait_ge(x_lo_dve, t + 1)
                    else:
                        pe.wait_ge(x_lo_pool, t - DVE_X_TILES + 1)
                    xh = x_of(x_hi, t).rearrange("p (c n) -> p c n", c=FC)
                    xl = x_of(x_lo, t).rearrange("p (c n) -> p c n", c=FC)
                    for c in range(FC):
                        if t == 0 and c % 2 == 0:
                            pe.wait_ge(wl_lo_ready, c // 2 + 1)
                        three(h, xh[:, c, :], xl[:, c, :], wl_hi[:, c, :], wl_lo[:, c, :], c == 0, False)
                    if t == 0:
                        pe.wait_ge(table_ready, 1)
                        pe.wait_ge(onehot_ready, 1)
                    nc.tensor.matmul(h, onehot[0:TABLE_ROWS, t0:t0 + n], table[0:TABLE_ROWS, :], start=False,
                                     stop=True, skip_group_check=True).then_inc(embedded, 1)
                elif stage == "T1":
                    n = TILE[t][1]
                    if t == 0:
                        pe.wait_ge(small_in, 16)
                    pe.wait_ge(xn1_ready, t + 1)
                    for c in range(DC):
                        ins = nc.tensor.transpose(turn_bank[:, c * P:c * P + n], xn1[0:n, t, c * P:(c + 1) * P],
                                                  ident[0:n, 0:n])
                    ins.then_inc(xn1_turned, 1)
                elif stage == "QK":
                    t0, n = TILE[t]
                    pe.wait_ge(xn1_t_ready, t + 1)
                    for m in range(2):
                        for c in range(DC):
                            ins = nc.tensor.matmul(mix_bank[:, m * P:m * P + n], wqkv[:, c, m, :],
                                                   xn1_t[:, c, t0:t0 + n], start=c == 0, stop=c == DC - 1)
                    ins.then_inc(qk_done, 1)
                elif stage == "VS":
                    t0, n = SPAN[t]
                    pe.wait_ge(qk_ready, 2 * ((t0 + n - 1) // P + 1))
                    if t == GROUPS - 1:
                        pe.wait_ge(v_ready, t)
                        pe.wait_ge(s_ready, t)
                    for c in range(DC):
                        nc.tensor.matmul(mix_bank[0:n, 0:HEAD], xn1_t[:, c, t0:t0 + n], wqkv[:, c, 2, :],
                                         start=c == 0, stop=c == DC - 1)
                    nc.tensor.matmul(mix_bank[0:n, HEAD:HEAD + n], q_t[:, t0:t0 + n], k_t[:, t0:t0 + n],
                                     start=True, stop=True).then_inc(vs_done, 1)
                elif stage == "PT":
                    n = SPAN[t][1]
                    pe.wait_ge(probs_n_ready, t + 1)
                    nc.tensor.transpose(turn_bank[0:n, 0:n], probs_n[0:n, t, 0:n],
                                        ident[0:n, 0:n]).then_inc(probs_turned, 1)
                elif stage == "OT":
                    n = SPAN[t][1]
                    pe.wait_ge(probs_t_ready, t + 1)
                    pe.wait_ge(v_ready, t + 1)
                    nc.tensor.matmul(mix_bank[:, 0:n], v[0:n, t, :], probs_t[0:n, t, 0:n],
                                     start=True, stop=True).then_inc(o_done, 1)
                elif stage == "O":
                    t0, n = TILE[t]
                    h = h_bank[t % H_BANKS][0:n, 0:D]
                    pe.wait_ge(o_t_ready, (t0 + n - 1) // GROUP + 1)
                    if t == 0:
                        pe.wait_ge(ones_ready, 1)
                        pe.wait_ge(bias_tables_ready, 1)
                    nc.tensor.matmul(h, o_t[:, t0:t0 + n], col("wo"), start=False, stop=False, skip_group_check=True)
                    nc.tensor.matmul(h, ones[0:BO_ROWS, 0:n], bo[0:BO_ROWS, :], start=False, stop=True,
                                     skip_group_check=True).then_inc(projected, 1)
                elif stage == "T2":
                    n = TILE[t][1]
                    pe.wait_ge(xn2_ready, t + 1)
                    for c in range(DC):
                        ins = nc.tensor.transpose(turn_bank[:, c * P:c * P + n], xn2[0:n, t, c * P:(c + 1) * P],
                                                  ident[0:n, 0:n])
                    ins.then_inc(xn2_turned, 1)
                elif stage == "G":
                    n = TILE[t][1]
                    pe.wait_ge(xn2_t_ready, t + 1)
                    for c in range(DC):
                        ins = nc.tensor.matmul(mix_bank[0:n, 0:EXPERTS], xn2_t[:, t, c, 0:n], gate_w[:, c, :],
                                               start=c == 0, stop=c == DC - 1)
                    ins.then_inc(gate_done, 1)
                elif stage == "B":
                    n = TILE[t][1]
                    pe.wait_ge(weights_ready, 2 * (t + 1))
                    nc.tensor.transpose(turn_bank[0:EB_ROWS, 0:n], w_stack[0:n, t, :].bitcast(F32),
                                        ident[0:n, 0:n]).then_inc(weights_turned, 1)
                    if t == 0:
                        pe.wait_ge(bias_tables_ready, 2)
                    pe.wait_ge(w_stack_t_ready, t + 1)
                    nc.tensor.matmul(h_bank[t % H_BANKS][0:n, 0:D], w_stack_t[0:EB_ROWS, t, 0:n], eb[0:EB_ROWS, :],
                                     start=False, stop=True, skip_group_check=True).then_inc(biased, 1)
                elif stage[0] == "Y":
                    n, q = TILE[t][1], stage[1]
                    i = QUARTERS * t + q
                    bank = y_bank[i % Y_BANKS][0:n, :]
                    if i >= Y_BANKS:
                        j = i - Y_BANKS
                        if j % QUARTERS == QUARTERS - 1:
                            pe.wait_ge(out_ready, j // QUARTERS + 1)
                        else:
                            pe.wait_ge(y_used, j + 1 - j // QUARTERS)
                    if t == 0:
                        if q < DVE_QUARTERS:
                            pe.wait_ge(ew_lo_dve, q + 1)
                        else:
                            pe.wait_ge(ew_lo_pool, DC * (q - DVE_QUARTERS + 1))
                    pe.wait_ge(xn2_lo_ready, t + 1)
                    for c in range(DC):
                        ins = three(bank, xn2_hi[:, t, c, 0:n], xn2_lo[:, t, c, 0:n], ew_hi[:, q, c, :],
                                    ew_lo[:, q, c, :], c == 0, c == DC - 1)
                    ins.then_inc(y_done, 1)


def kernel(**inputs):
    import numpy as np
    import concourse.bacc as bacc
    from concourse.bass_utils import run_bass_kernel_spmd

    a = {k: np.asarray(x) for k, x in inputs.items()}
    f32 = np.float32

    patches = a["x"].reshape(IMAGES, CHANNELS, GRID, PATCH, GRID, PATCH).transpose(1, 3, 5, 0, 2, 4)
    cols = np.zeros((F, IMAGES, SEQ), f32)
    cols[:, :, 2:] = patches.reshape(F, IMAGES, SEQ - 2)
    cols = cols.reshape(FC, P, TOKENS).transpose(1, 0, 2)
    x_t = np.concatenate([cols[:, :, t0:t0 + n].reshape(P, FC * n) for t0, n in TILE], axis=1)
    w_lin_t = a["L0_tok_W_lin"].T.reshape(FC, P, D).transpose(1, 0, 2)
    expert_w = a["L0_ffn_expert_w"].reshape(QUARTERS, PER_QUARTER, DC, P, D).transpose(3, 0, 2, 1, 4)

    small = np.zeros((P, SMALL), f32)

    def put(name, block, row=0):
        block = block.reshape(block.shape[0], -1)
        small[row:row + block.shape[0], COL[name][0]:COL[name][1]] = block

    position = a["L0_tok_position_embeddings"][0]
    table_a = np.concatenate([a["cls_tok"][0], position])
    table_b = np.zeros((SEQ, D), f32)
    table_b[1] = a["L0_tok_class_token"][0, 0]
    table_b[2:] = a["L0_tok_b_lin"]
    onehot = np.tile(np.eye(SEQ, dtype=f32), (1, IMAGES))
    for row in (0, TABLE_LO):
        put("table_a", table_a, row)
        put("table_b", table_b, row)
        put("onehot", onehot, row)
    put("ident", np.eye(P, dtype=f32))
    wqkv = np.stack([a["L0_attn_W" + m].T.reshape(DC, P, HEAD) for m in "qkv"])
    put("wqkv", wqkv.transpose(2, 1, 0, 3))
    put("biases", np.stack([a["L0_attn_b" + m] for m in "qkv"], axis=1))
    r = np.arange(GROUP)
    is_open = (r[:, None] // SEQ == r[None, :] // SEQ) & (r[:, None] >= r[None, :])
    put("mask", np.where(is_open, f32(0), f32(CLOSED)))
    put("wo", a["L0_attn_Wo"].T)
    for row in (0, 32):
        put("bo", a["L0_attn_bo"][None], row)
    put("gate_w", a["L0_ffn_gate_w"].reshape(DC, P, EXPERTS).transpose(1, 0, 2))
    put("gate_b", np.broadcast_to(a["L0_ffn_gate_b"], (P, EXPERTS)))
    for row in (0, 32, 64):
        put("expert_b", a["L0_ffn_expert_b"], row)

    arrays = {"x_t": x_t, "w_lin_t": w_lin_t, "small": small, "expert_w": expert_w.reshape(P, QUARTERS, DC, BANK)}
    arrays = {k: np.ascontiguousarray(x) for k, x in arrays.items()}
    nc = bacc.Bacc("TRN2", target_bir_lowering=False, num_devices=1)
    args = [nc.dram_tensor(k, x.shape, F32, kind="ExternalInput").ap() for k, x in arrays.items()]
    args.append(nc.dram_tensor("out", (TOKENS, D), F32, kind="ExternalOutput").ap())
    build(nc, *args)
    res = run_bass_kernel_spmd(nc, [arrays], core_ids=[0])
    return res.results[0]["out"].reshape(IMAGES, SEQ, D)
```

```python
from contextlib import ExitStack

import concourse.bass as bass
from concourse import mybir

F32 = mybir.dt.float32
F32R = mybir.dt.float32r
ALU = mybir.AluOpType
ACT = mybir.ActivationFunctionType

P = 128
IMAGES, CHANNELS, SIDE, PATCH = 16, 3, 96, 16
GRID = SIDE // PATCH
SEQ = GRID * GRID + 2
TOKENS = IMAGES * SEQ
D = 256
DC = D // P
F = CHANNELS * PATCH * PATCH
FC = F // P
HEAD = 128
EXPERTS = 8
THRESHOLD = 0.1
EPS = 1e-5
TILES = -(-TOKENS // P)
IMAGES_PER_GROUP = P // SEQ
GROUP = IMAGES_PER_GROUP * SEQ
GROUPS = -(-TOKENS // GROUP)
BANK = 512
QUARTERS = EXPERTS * D // BANK
PER_QUARTER = EXPERTS // QUARTERS
MISC_BANKS, Y_BANKS = 5, 3
WL_PARTS = 3
CLOSED = -1.0e30

TABLE_LO = 64
TABLE_ROWS = TABLE_LO + SEQ
BO_ROWS = 33
EB_ROWS = 64 + EXPERTS

TILE = [(P * t, min(P, TOKENS - P * t)) for t in range(TILES)]
SPAN = [(GROUP * g, min(GROUP, TOKENS - GROUP * g)) for g in range(GROUPS)]

ONEHOT = SEQ + P

def _columns(*widths):
    at, n = {}, 0
    for name, width in widths:
        at[name] = (n, n + width)
        n += width
    return at, n


FIRST_COL, FIRST_SMALL = _columns(("table_a", D), ("table_b", D), ("onehot", ONEHOT))
COL, SMALL = _columns(("ident", P), ("wqkv", DC * 3 * HEAD), ("biases", 3), ("mask", GROUP), ("wo", D), ("bo", D),
                      ("gate_w", DC * EXPERTS), ("gate_b", EXPERTS), ("expert_b", D))

ORDER = {
    "tensor": (
        "embed.0 embed.1 embed.2 turn1.0 turn1.1 qk.0 qk.1 embed.3 turn1.2 scores.0 scores.1 v.0 v.1 v.2 "
        "qk.2 embed.4 turn1.3 scores.2 turnp.0 turnp.1 qk.3 v.3 pv.0 turnp.2 pv.1 scores.3 turn1.4 pv.2 "
        "project.0 qk.4 v.4 v.5 project.1 turnp.3 scores.4 scores.5 turn2.0 pv.3 gate.0 project.2 "
        "turn2.1 turnp.4 gate.1 pv.4 expert.0 project.3 turn2.2 turnw.0 expert.1 expert.2 bias.0 "
        "expert.3 turn2.3 turnp.5 turnw.1 gate.2 expert.4 pv.5 bias.1 expert.5 project.4 expert.6 "
        "turnw.2 expert.7 bias.2 gate.3 expert.8 turn2.4 expert.9 expert.10 expert.11 turnw.3 gate.4 "
        "expert.12 bias.3 expert.13 expert.14 expert.15 turnw.4 expert.16 bias.4 expert.17 expert.18 "
        "expert.19"),
    "scalar": (
        "wl_hi.0 x_hi.0 wl_hi.1 wl_hi.2 onehot.0 x_hi.1 x_hi.2 copy_h.0 ew_hi.0 copy_h.1 ew_hi.1 ew_hi.2 "
        "ew_hi.3 x_hi.3 copy_h.2 copy_x1.0 copy_x1.1 ew_hi.4 ew_hi.5 copy_qk.0 ew_hi.6 copy_qk.1 x_hi.4 "
        "ew_hi.7 copy_h.3 copy_x1.2 exp.0 copy_v.0 exp.1 copy_v.1 copy_v.2 copy_qk.2 copy_h.4 copy_x1.3 "
        "copy_p.0 copy_p.1 exp.2 copy_qk.3 copy_v.3 copy_o.0 copy_p.2 copy_o.1 copy_x1.4 copy_o.2 exp.3 "
        "copy_qk.4 copy_v.4 copy_v.5 copy_p.3 copy_x2.0 copy_o.3 exp.4 exp.5 gate_exp.0 copy_x2.1 "
        "copy_p.4 copy_o.4 gate_exp.1 scale_y.0 copy_x2.2 copy_w.0 copy_x2.3 copy_p.5 copy_w.1 "
        "gate_exp.2 scale_y.1 copy_o.5 copy_w.2 scale_y.2 gate_exp.3 copy_x2.4 copy_w.3 scale_y.3 "
        "gate_exp.4 copy_w.4 scale_y.4"),
    "vector": (
        "wl_lo.0 x_lo.0 wl_lo.1 wl_lo.2 table.0 x_lo.1 bias_tables.0 stats1.0 ew_lo.0 stats1.1 norm1.0 "
        "ew_lo.1 norm1.1 ew_lo.2 ew_lo.3 stats1.2 norm1.2 max.0 max.1 stats1.3 norm_p.0 norm_p.1 norm1.3 "
        "max.2 stats1.4 norm_p.2 norm1.4 max.3 stats2.0 norm_p.3 norm2.0 stats2.1 max.4 max.5 norm2.1 "
        "logits.0 norm_p.4 stats2.2 x2_lo.0 x2_lo.1 logits.1 norm2.2 weights.0 weights.1 stats2.3 "
        "x2_lo.2 norm_p.5 start_acc.0 norm2.3 add_y.1 add_y.2 logits.2 x2_lo.3 add_y.3 weights.2 "
        "stats2.4 start_acc.1 add_y.5 norm2.4 add_y.6 logits.3 add_y.7 weights.3 x2_lo.4 start_acc.2 "
        "add_y.9 add_y.10 logits.4 add_y.11 weights.4 start_acc.3 add_y.13 add_y.14 add_y.15 start_acc.4 "
        "add_y.17 add_y.18 add_y.19"),
    "gpsimd": (
        "x_lo.2 rstd1.0 rstd1.1 x_lo.3 rstd1.2 ew_lo.4 ew_lo.5 x_lo.4 ew_lo.6 rstd1.3 ew_lo.7 rstd1.4 "
        "rstd2.0 rstd2.1 rstd2.2 add_scaled.0 rstd2.3 add_scaled.1 rstd2.4 add_scaled.2 add_scaled.3 "
        "add_scaled.4"),
}

X_LOW = {t: "vector" if f"x_lo.{t}" in ORDER["vector"].split() else "gpsimd" for t in range(TILES)}
EW_LOW = {i: "vector" if f"ew_lo.{i}" in ORDER["vector"].split() else "gpsimd" for i in range(QUARTERS * DC)}


def steps_of(engine):
    for word in ORDER[engine].split():
        stage, index = word.split(".")
        yield stage, int(index)


MISC_USE = {step: use for use, step in enumerate(s for s in steps_of("tensor") if s[0] != "expert")}


def count_of(owner, engine, i):
    return sum(owner[j] == engine for j in range(i + 1))


def build(nc, x_t, w_lin_t, first_small, small, expert_w, out):
    ctx = ExitStack()
    with ctx:
        def sb(name, shape, dt=F32):
            return ctx.enter_context(nc.sbuf_tensor(name, shape, dt))

        def psum(name):
            return ctx.enter_context(nc.psum_tensor(name, [P, BANK], F32))

        def sem(name):
            return ctx.enter_context(nc.semaphore(name))

        x_raw = sb("x_raw", [P, FC * TOKENS])
        x_hi = sb("x_hi", [P, FC * TOKENS], F32R)
        x_lo = sb("x_lo", [P, FC * TOKENS], F32R)
        wl_raw = sb("wl_raw", [P, FC, D])
        wl_hi = sb("wl_hi", [P, FC, D], F32R)
        wl_lo = sb("wl_lo", [P, FC, D], F32R)
        ew_raw = sb("ew_raw", [P, QUARTERS * DC, BANK])
        ew_hi = sb("ew_hi", [P, QUARTERS * DC, BANK], F32R)
        ew_lo = sb("ew_lo", [P, QUARTERS * DC, BANK], F32R)
        first_sm = sb("first_sm", [P, FIRST_SMALL])
        sm = sb("sm", [P, SMALL])
        table_sum = sb("table_sum", [P, D])
        table = sb("table", [P, D], F32R)
        onehot = sb("onehot", [P, ONEHOT], F32R)
        ones = sb("ones", [P, P], F32R)
        bo = sb("bo", [P, D], F32R)
        eb = sb("eb", [P, D], F32R)
        hidden = sb("hidden", [P, 2, TILES, D])
        stats = sb("stats", [P, 2, TILES, 6])
        moments = sb("moments", [P, 2, TILES, 2])
        var_eps = sb("var_eps", [P, 2, TILES, 1])
        minus_half = sb("minus_half", [P, 1])
        rstd = sb("rstd", [P, 2, TILES, 1])
        xn = sb("xn", [P, 2, TILES, D])
        xn1_t = sb("xn1_t", [P, DC, TOKENS])
        q_t = sb("q_t", [P, TOKENS])
        k_t = sb("k_t", [P, TOKENS])
        v = sb("v", [P, GROUPS, HEAD])
        scores = sb("scores", [P, GROUPS, GROUP])
        row_max = sb("row_max", [P, GROUPS])
        exp_bias = sb("exp_bias", [P, GROUPS])
        row_sum = sb("row_sum", [P, GROUPS])
        row_inv = sb("row_inv", [P, GROUPS])
        probs = sb("probs", [P, GROUPS, GROUP])
        probs_n = sb("probs_n", [P, GROUPS, GROUP])
        probs_t = sb("probs_t", [P, GROUPS, GROUP])
        o_t = sb("o_t", [P, TOKENS])
        xn2_t = sb("xn2_t", [P, TILES, DC, P])
        xn2_hi = sb("xn2_hi", [P, TILES, DC, P], F32R)
        xn2_lo = sb("xn2_lo", [P, TILES, DC, P], F32R)
        logits = sb("logits", [P, TILES, EXPERTS])
        gate_exp = sb("gate_exp", [P, TILES, EXPERTS])
        picked = sb("picked", [P, TILES, EXPERTS])
        weights = sb("weights", [P, TILES, EXPERTS])
        gate_cols = sb("gate_cols", [P, TILES, 8])
        w_stack = sb("w_stack", [P, TILES, EB_ROWS], F32R)
        w_stack_t = sb("w_stack_t", [P, TILES, P], F32R)
        scaled = sb("scaled", [P, TILES, PER_QUARTER, D])
        acc = sb("acc", [P, TILES, D])

        misc = [psum(f"misc{i}") for i in range(MISC_BANKS)]
        y_bank = [psum(f"y_bank{i}") for i in range(Y_BANKS)]

        def col(name, rows=P):
            return sm[0:rows, COL[name][0]:COL[name][1]]

        def first_col(name):
            return first_sm[0:TABLE_ROWS, FIRST_COL[name][0]:FIRST_COL[name][1]]

        ident = col("ident")
        wqkv = col("wqkv").rearrange("p (c m h) -> p c m h", c=DC, m=3)
        gate_w = col("gate_w").rearrange("p (c e) -> p c e", c=DC)

        def x_of(buf, t):
            t0, n = TILE[t]
            return buf[:, FC * t0:FC * (t0 + n)]

        def bank_of(stage, i):
            return misc[MISC_USE[(stage, i)] % MISC_BANKS]

        wl_in = [sem(f"wl_in{i}") for i in range(WL_PARTS)]
        x_in = [sem(f"x_in{t}") for t in range(TILES)]
        table_in, small_in = sem("table_in"), sem("small_in")
        ew_in = [sem(f"ew_in{q}") for q in range(QUARTERS)]
        out_stored = sem("out_stored")
        wl_hi_ready, wl_lo_ready = sem("wl_hi_ready"), sem("wl_lo_ready")
        x_hi_ready = sem("x_hi_ready")
        x_lo_ready = {e: sem(f"x_lo_{e}") for e in ("vector", "gpsimd")}
        table_ready, onehot_ready, ones_ready = sem("table_ready"), sem("onehot_ready"), sem("ones_ready")
        bias_tables_ready, stack_cleared, half_ready = sem("bias_tables_ready"), sem("stack_cleared"), sem("half_ready")
        ew_hi_ready = sem("ew_hi_ready")
        ew_lo_ready = {e: sem(f"ew_lo_{e}") for e in ("vector", "gpsimd")}
        dve_step, pool_step = sem("dve_step"), sem("pool_step")
        embedded, h_ready, projected, h2_ready = sem("embedded"), sem("h_ready"), sem("projected"), sem("h2_ready")
        var_ready = [sem("var1_ready"), sem("var2_ready")]
        rstd_ready = [sem("rstd1_ready"), sem("rstd2_ready")]
        xn_ready = [sem("xn1_ready"), sem("xn2_ready")]
        xn1_turned, xn1_t_ready = sem("xn1_turned"), sem("xn1_t_ready")
        qk_done, qk_ready, v_done, v_ready = sem("qk_done"), sem("qk_ready"), sem("v_done"), sem("v_ready")
        scores_done, scores_ready, exp_bias_ready = sem("scores_done"), sem("scores_ready"), sem("exp_bias_ready")
        probs_ready, probs_n_ready = sem("probs_ready"), sem("probs_n_ready")
        probs_turned, probs_t_ready = sem("probs_turned"), sem("probs_t_ready")
        pv_done, o_t_ready = sem("pv_done"), sem("o_t_ready")
        xn2_turned, xn2_t_ready, xn2_lo_ready = sem("xn2_turned"), sem("xn2_t_ready"), sem("xn2_lo_ready")
        gate_done, logits_ready = sem("gate_done"), sem("logits_ready")
        gate_max_ready, gate_exp_ready = sem("gate_max_ready"), sem("gate_exp_ready")
        weights_ready, w_stack_ready = sem("weights_ready"), sem("w_stack_ready")
        weights_turned, w_stack_t_ready = sem("weights_turned"), sem("w_stack_t_ready")
        biased, acc_ready = sem("biased"), sem("acc_ready")
        y_done, y_scaled, start_ready, y_added = sem("y_done"), sem("y_scaled"), sem("start_ready"), sem("y_added")

        last_reader = {"embed": (h_ready, 1), "turn1": (xn1_t_ready, 1), "qk": (qk_ready, 2), "v": (v_ready, 1),
                       "scores": (scores_ready, 1), "turnp": (probs_t_ready, 1), "pv": (o_t_ready, 1),
                       "project": (h2_ready, 1), "turn2": (xn2_t_ready, 2), "gate": (logits_ready, 1),
                       "turnw": (w_stack_t_ready, 1), "bias": (acc_ready, 1)}

        block = ctx.enter_context(nc.Block())

        @block.sync
        def _(sp):
            def load_x(t):
                sp.dma_start(x_of(x_raw, t), x_of(x_t, t)).then_inc(x_in[t], 16)

            def load_wl(i):
                c = slice(FC // WL_PARTS * i, FC // WL_PARTS * (i + 1))
                sp.dma_start(wl_raw[:, c, :], w_lin_t[:, c, :]).then_inc(wl_in[i], 16)

            def load_ew(q):
                c = slice(DC * q, DC * (q + 1))
                sp.dma_start(ew_raw[:, c, :], expert_w[:, c, :]).then_inc(ew_in[q], 16)

            load_wl(0)
            load_x(0)
            for i in range(1, WL_PARTS):
                load_wl(i)
            sp.dma_start(first_sm[0:TABLE_ROWS, :], first_small).then_inc(table_in, 16)
            load_x(1)
            sp.dma_start(sm[:], small).then_inc(small_in, 16)
            load_x(2)
            load_ew(0)
            load_ew(1)
            load_x(3)
            load_ew(2)
            load_ew(3)
            load_x(4)
            for t in range(TILES):
                t0, n = TILE[t]
                sp.wait_ge(y_added, (QUARTERS - 1) * (t + 1))
                sp.dma_start(out[t0:t0 + n, :], acc[0:n, t, :]).then_inc(out_stored, 16)
            sp.wait_ge(out_stored, 16 * TILES)

        @block.gpsimd
        def _(pool):
            nc.gpsimd.memset(minus_half[:], -0.5).then_inc(half_ready, 1)
            pool.wait_ge(half_ready, 1)

            for stage, i in steps_of("gpsimd"):
                if stage == "x_lo":
                    pool.wait_ge(x_hi_ready, i + 1)
                    nc.gpsimd.tensor_tensor(x_of(x_lo, i), x_of(x_raw, i), x_of(x_hi, i).bitcast(F32),
                                            ALU.subtract).then_inc(x_lo_ready["gpsimd"], 1)
                elif stage == "ew_lo":
                    pool.wait_ge(ew_hi_ready, i + 1)
                    nc.gpsimd.tensor_tensor(ew_lo[:, i, :], ew_raw[:, i, :], ew_hi[:, i, :].bitcast(F32),
                                            ALU.subtract).then_inc(ew_lo_ready["gpsimd"], 1)
                elif stage in ("rstd1", "rstd2"):
                    which, n = int(stage[-1]) - 1, TILE[i][1]
                    pool.wait_ge(var_ready[which], i + 1)
                    nc.gpsimd.tensor_tensor(rstd[0:n, which, i, :], var_eps[0:n, which, i, :], minus_half[0:n, :],
                                            ALU.pow).then_inc(rstd_ready[which], 1)
                elif stage == "add_scaled":
                    n = TILE[i][1]
                    pool.wait_ge(y_scaled, PER_QUARTER * (i + 1))
                    total = scaled[0:n, i, 0, :]
                    nc.gpsimd.tensor_tensor(total, total, scaled[0:n, i, 1, :],
                                            ALU.add).then_inc(pool_step, 1)
                    pool.wait_ge(pool_step, i + 1)
                    pool.wait_ge(h2_ready, i + 1)
                    nc.gpsimd.tensor_tensor(total, total, hidden[0:n, 1, i, :],
                                            ALU.add).then_inc(start_ready, 1)

        @block.scalar
        def _(act):
            for stage, i in steps_of("scalar"):
                if stage == "wl_hi":
                    c = slice(FC // WL_PARTS * i, FC // WL_PARTS * (i + 1))
                    act.wait_ge(wl_in[i], 16)
                    nc.scalar.copy(wl_hi[:, c, :], wl_raw[:, c, :]).then_inc(wl_hi_ready, 1)
                elif stage == "x_hi":
                    act.wait_ge(x_in[i], 16)
                    nc.scalar.copy(x_of(x_hi, i), x_of(x_raw, i)).then_inc(x_hi_ready, 1)
                elif stage == "onehot":
                    act.wait_ge(table_in, 16)
                    nc.scalar.copy(onehot[0:TABLE_ROWS, :], first_col("onehot")).then_inc(onehot_ready, 1)
                elif stage == "ew_hi":
                    act.wait_ge(ew_in[i // DC], 16)
                    nc.scalar.copy(ew_hi[:, i, :], ew_raw[:, i, :]).then_inc(ew_hi_ready, 1)
                elif stage == "copy_h":
                    n = TILE[i][1]
                    act.wait_ge(embedded, i + 1)
                    nc.scalar.copy(hidden[0:n, 0, i, :], bank_of("embed", i)[0:n, 0:D]).then_inc(h_ready, 1)
                elif stage == "copy_x1":
                    t0, n = TILE[i]
                    act.wait_ge(xn1_turned, i + 1)
                    nc.scalar.copy(xn1_t[:, :, t0:t0 + n],
                                   bank_of("turn1", i)[:, 0:D].rearrange("p (c n) -> p c n", c=DC)[:, :, 0:n]
                                   ).then_inc(xn1_t_ready, 1)
                elif stage == "copy_qk":
                    t0, n = TILE[i]
                    if i == 0:
                        act.wait_ge(small_in, 16)
                    act.wait_ge(qk_done, i + 1)
                    for m, to in enumerate((q_t, k_t)):
                        nc.scalar.activation(to[:, t0:t0 + n], bank_of("qk", i)[:, m * P:m * P + n], ACT.Identity,
                                             bias=col("biases")[:, m:m + 1]).then_inc(qk_ready, 1)
                elif stage == "copy_v":
                    n = SPAN[i][1]
                    act.wait_ge(v_done, i + 1)
                    nc.scalar.copy(v[0:n, i, :], bank_of("v", i)[0:n, 0:HEAD]).then_inc(v_ready, 1)
                elif stage == "exp":
                    n = SPAN[i][1]
                    act.wait_ge(exp_bias_ready, i + 1)
                    nc.scalar.activation(probs[0:n, i, 0:n], scores[0:n, i, 0:n], ACT.Exp,
                                         bias=exp_bias[0:n, i:i + 1], scale=float(HEAD) ** -0.5,
                                         accum_out=row_sum[0:n, i:i + 1]).then_inc(probs_ready, 1)
                elif stage == "copy_p":
                    n = SPAN[i][1]
                    act.wait_ge(probs_turned, i + 1)
                    nc.scalar.copy(probs_t[0:n, i, 0:n], bank_of("turnp", i)[0:n, 0:n]).then_inc(probs_t_ready, 1)
                elif stage == "copy_o":
                    t0, n = SPAN[i]
                    act.wait_ge(pv_done, i + 1)
                    nc.scalar.activation(o_t[:, t0:t0 + n], bank_of("pv", i)[:, 0:n], ACT.Identity,
                                         bias=col("biases")[:, 2:3]).then_inc(o_t_ready, 1)
                elif stage == "copy_x2":
                    n = TILE[i][1]
                    act.wait_ge(xn2_turned, i + 1)
                    src = bank_of("turn2", i)[:, 0:D].rearrange("p (c n) -> p c n", c=DC)[:, :, 0:n]
                    for to in (xn2_hi, xn2_t):
                        nc.scalar.copy(to[:, i, :, 0:n], src).then_inc(xn2_t_ready, 1)
                elif stage == "gate_exp":
                    n = TILE[i][1]
                    act.wait_ge(gate_max_ready, i + 1)
                    nc.scalar.activation(gate_exp[0:n, i, :], logits[0:n, i, :], ACT.Exp,
                                         bias=gate_cols[0:n, i, 1:2],
                                         accum_out=gate_cols[0:n, i, 2:3]).then_inc(gate_exp_ready, 1)
                elif stage == "copy_w":
                    n = TILE[i][1]
                    act.wait_ge(weights_turned, i + 1)
                    nc.scalar.copy(w_stack_t[0:EB_ROWS, i, 0:n],
                                   bank_of("turnw", i)[0:EB_ROWS, 0:n]).then_inc(w_stack_t_ready, 1)
                elif stage == "scale_y":
                    n, y = TILE[i][1], QUARTERS * i
                    act.wait_ge(weights_ready, i + 1)
                    act.wait_ge(y_done, y + 1)
                    for e in range(PER_QUARTER):
                        nc.scalar.activation(scaled[0:n, i, e, :], y_bank[y % Y_BANKS][0:n, e * D:(e + 1) * D],
                                             ACT.Copy, scale=weights[0:n, i, e:e + 1]).then_inc(y_scaled, 1)

        @block.vector
        def _(dve):
            steps = [0]

            def then(ins):
                steps[0] += 1
                ins.then_inc(dve_step, 1)
                dve.wait_ge(dve_step, steps[0])

            def low(out_ap, raw, hi):
                return nc.vector.tensor_tensor(out_ap, raw, hi.bitcast(F32), ALU.subtract)

            def norm_stats(which, t):
                n = TILE[t][1]
                then(nc.vector.bn_stats(stats[0:n, which, t, :], hidden[0:n, which, t, :]))
                then(nc.vector.bn_aggr(moments[0:n, which, t, :], stats[0:n, which, t, :]))
                nc.vector.tensor_scalar_add(var_eps[0:n, which, t, :], moments[0:n, which, t, 1:2],
                                            EPS).then_inc(var_ready[which], 1)

            nc.vector.memset(ones[:].bitcast(F32), 1.0).then_inc(ones_ready, 1)
            nc.vector.memset(w_stack[:].bitcast(F32), 0.0).then_inc(stack_cleared, 1)
            dve.wait_ge(stack_cleared, 1)

            for stage, i in steps_of("vector"):
                if stage == "wl_lo":
                    c = slice(FC // WL_PARTS * i, FC // WL_PARTS * (i + 1))
                    dve.wait_ge(wl_hi_ready, i + 1)
                    low(wl_lo[:, c, :], wl_raw[:, c, :], wl_hi[:, c, :]).then_inc(wl_lo_ready, 1)
                elif stage == "x_lo":
                    dve.wait_ge(x_hi_ready, i + 1)
                    low(x_of(x_lo, i), x_of(x_raw, i), x_of(x_hi, i)).then_inc(x_lo_ready["vector"], 1)
                elif stage == "ew_lo":
                    dve.wait_ge(ew_hi_ready, i + 1)
                    low(ew_lo[:, i, :], ew_raw[:, i, :], ew_hi[:, i, :]).then_inc(ew_lo_ready["vector"], 1)
                elif stage == "table":
                    dve.wait_ge(table_in, 16)
                    then(nc.vector.tensor_tensor(table_sum[0:TABLE_ROWS, :], first_col("table_a"), first_col("table_b"),
                                                 ALU.add))
                    then(nc.vector.tensor_copy(table[0:TABLE_ROWS, :], table_sum[0:TABLE_ROWS, :]))
                    rows = slice(TABLE_LO, TABLE_ROWS)
                    low(table[rows, :], table_sum[rows, :], table[rows, :]).then_inc(table_ready, 1)
                elif stage == "bias_tables":
                    dve.wait_ge(small_in, 16)
                    then(nc.vector.tensor_copy(bo[0:BO_ROWS, :], col("bo", BO_ROWS)))
                    low(bo[32:33, :], sm[32:33, COL["bo"][0]:COL["bo"][1]], bo[32:33, :]).then_inc(bias_tables_ready, 1)
                    then(nc.vector.tensor_copy(eb[0:EB_ROWS, :], col("expert_b", EB_ROWS)))
                    rows = slice(32, 32 + EXPERTS)
                    low(eb[rows, :], sm[rows, COL["expert_b"][0]:COL["expert_b"][1]],
                        eb[rows, :]).then_inc(bias_tables_ready, 1)
                elif stage == "stats1":
                    dve.wait_ge(h_ready, i + 1)
                    norm_stats(0, i)
                elif stage in ("norm1", "norm2"):
                    which, n = int(stage[-1]) - 1, TILE[i][1]
                    dve.wait_ge(rstd_ready[which], i + 1)
                    nc.vector.tensor_scalar(xn[0:n, which, i, :], hidden[0:n, which, i, :],
                                            moments[0:n, which, i, 0:1], rstd[0:n, which, i, :],
                                            ALU.subtract, ALU.mult).then_inc(xn_ready[which], 1)
                elif stage == "max":
                    n = SPAN[i][1]
                    dve.wait_ge(scores_done, i + 1)
                    nc.vector.tensor_tensor_reduce(out=scores[0:n, i, 0:n], in0=bank_of("scores", i)[0:n, 0:n],
                                                   in1=col("mask")[0:n, 0:n], scale=1.0, scalar=-3.0e38,
                                                   op0=ALU.add, op1=ALU.max,
                                                   accum_out=row_max[0:n, i:i + 1]).then_inc(scores_ready, 1)
                    dve.wait_ge(scores_ready, i + 1)
                    nc.vector.tensor_scalar(exp_bias[0:n, i:i + 1], row_max[0:n, i:i + 1],
                                            -float(HEAD) ** -0.5, None, ALU.mult).then_inc(exp_bias_ready, 1)
                elif stage == "norm_p":
                    n = SPAN[i][1]
                    dve.wait_ge(probs_ready, i + 1)
                    then(nc.vector.reciprocal(row_inv[0:n, i:i + 1], row_sum[0:n, i:i + 1]))
                    nc.vector.tensor_scalar(probs_n[0:n, i, 0:n], probs[0:n, i, 0:n], row_inv[0:n, i:i + 1], None,
                                            ALU.mult).then_inc(probs_n_ready, 1)
                elif stage == "stats2":
                    n = TILE[i][1]
                    dve.wait_ge(projected, i + 1)
                    nc.vector.tensor_tensor(hidden[0:n, 1, i, :], bank_of("project", i)[0:n, 0:D],
                                            hidden[0:n, 0, i, :], ALU.add).then_inc(h2_ready, 1)
                    dve.wait_ge(h2_ready, i + 1)
                    norm_stats(1, i)
                elif stage == "x2_lo":
                    n = TILE[i][1]
                    dve.wait_ge(xn2_t_ready, 2 * (i + 1))
                    low(xn2_lo[:, i, :, 0:n], xn2_t[:, i, :, 0:n], xn2_hi[:, i, :, 0:n]).then_inc(xn2_lo_ready, 1)
                elif stage == "logits":
                    n = TILE[i][1]
                    dve.wait_ge(gate_done, i + 1)
                    nc.vector.tensor_tensor_reduce(out=logits[0:n, i, :], in0=bank_of("gate", i)[0:n, 0:EXPERTS],
                                                   in1=col("gate_b")[0:n, :], scale=1.0, scalar=-3.0e38,
                                                   op0=ALU.add, op1=ALU.max,
                                                   accum_out=gate_cols[0:n, i, 0:1]).then_inc(logits_ready, 1)
                    dve.wait_ge(logits_ready, i + 1)
                    nc.vector.tensor_scalar(gate_cols[0:n, i, 1:2], gate_cols[0:n, i, 0:1], -1.0, None,
                                            ALU.mult).then_inc(gate_max_ready, 1)
                elif stage == "weights":
                    n = TILE[i][1]
                    c = gate_cols[0:n, i, :]
                    dve.wait_ge(gate_exp_ready, i + 1)
                    then(nc.vector.tensor_scalar(c[:, 3:4], c[:, 2:3], THRESHOLD, None, ALU.mult))
                    then(nc.vector.scalar_tensor_tensor(out=picked[0:n, i, :], in0=gate_exp[0:n, i, :],
                                                        scalar=c[:, 3:4], in1=gate_exp[0:n, i, :], op0=ALU.is_ge,
                                                        op1=ALU.mult, accum_out=c[:, 4:5]))
                    then(nc.vector.scalar_tensor_tensor(out=c[:, 5:6], in0=c[:, 4:5], scalar=0.0, in1=c[:, 4:5],
                                                        op0=ALU.is_equal, op1=ALU.add))
                    then(nc.vector.reciprocal(c[:, 6:7], c[:, 5:6]))
                    nc.vector.tensor_scalar(weights[0:n, i, :], picked[0:n, i, :], c[:, 6:7], None,
                                            ALU.mult).then_inc(weights_ready, 1)
                    nc.vector.tensor_scalar(w_stack[0:n, i, 0:EXPERTS], picked[0:n, i, :], c[:, 6:7], None,
                                            ALU.mult).then_inc(w_stack_ready, 1)
                    nc.vector.tensor_scalar(w_stack[0:n, i, 32:32 + EXPERTS], picked[0:n, i, :], c[:, 6:7], None,
                                            ALU.mult).then_inc(w_stack_ready, 1)
                    dve.wait_ge(weights_ready, i + 1)
                    dve.wait_ge(w_stack_ready, 3 * i + 1)
                    low(w_stack[0:n, i, 64:64 + EXPERTS], weights[0:n, i, :],
                        w_stack[0:n, i, 0:EXPERTS]).then_inc(w_stack_ready, 1)
                elif stage == "start_acc":
                    n = TILE[i][1]
                    dve.wait_ge(biased, i + 1)
                    dve.wait_ge(start_ready, i + 1)
                    nc.vector.tensor_tensor(acc[0:n, i, :], bank_of("bias", i)[0:n, 0:D], scaled[0:n, i, 0, :],
                                            ALU.add).then_inc(acc_ready, 1)
                elif stage == "add_y":
                    t, q = divmod(i, QUARTERS)
                    n = TILE[t][1]
                    added = (QUARTERS - 1) * t + q - 1
                    if q == 1:
                        dve.wait_ge(acc_ready, t + 1)
                    else:
                        dve.wait_ge(y_added, added)
                    dve.wait_ge(y_done, i + 1)
                    for j in range(PER_QUARTER):
                        e = PER_QUARTER * q + j
                        ins = nc.vector.scalar_tensor_tensor(
                            out=acc[0:n, t, :], in0=y_bank[i % Y_BANKS][0:n, j * D:(j + 1) * D],
                            scalar=weights[0:n, t, e:e + 1], in1=acc[0:n, t, :], op0=ALU.mult, op1=ALU.add)
                        if j < PER_QUARTER - 1:
                            then(ins)
                    ins.then_inc(y_added, 1)

        @block.tensor
        def _(pe):
            misc_order = [None] * len(MISC_USE)
            for key, use in MISC_USE.items():
                misc_order[use] = key

            def take_bank(stage, i):
                use = MISC_USE[(stage, i)]
                if use >= MISC_BANKS:
                    last, j = misc_order[use - MISC_BANKS]
                    reader, count = last_reader[last]
                    pe.wait_ge(reader, count * (j + 1))
                return misc[use % MISC_BANKS]

            def three(out_ap, stat_hi, stat_lo, mov_hi, mov_lo, start, stop):
                nc.tensor.matmul(out_ap, stat_hi, mov_hi, start=start, stop=False)
                nc.tensor.matmul(out_ap, stat_hi, mov_lo, start=False, stop=False)
                return nc.tensor.matmul(out_ap, stat_lo, mov_hi, start=False, stop=stop)

            seen = {"small": False, "onehot": False}
            for stage, i in steps_of("tensor"):
                if stage == "embed":
                    t0, n = TILE[i]
                    h = take_bank(stage, i)[0:n, 0:D]
                    pe.wait_ge(x_lo_ready[X_LOW[i]], count_of(X_LOW, X_LOW[i], i))
                    xh = x_of(x_hi, i).rearrange("p (c n) -> p c n", c=FC)
                    xl = x_of(x_lo, i).rearrange("p (c n) -> p c n", c=FC)
                    for c in range(FC):
                        if i == 0 and c % (FC // WL_PARTS) == 0:
                            pe.wait_ge(wl_lo_ready, c // (FC // WL_PARTS) + 1)
                        three(h, xh[:, c, :], xl[:, c, :], wl_hi[:, c, :], wl_lo[:, c, :], c == 0, False)
                    if i == 0:
                        pe.wait_ge(table_ready, 1)
                        pe.wait_ge(onehot_ready, 1)
                    nc.tensor.matmul(h, onehot[0:TABLE_ROWS, t0 % SEQ:t0 % SEQ + n], table[0:TABLE_ROWS, :],
                                     start=False, stop=True).then_inc(embedded, 1)
                elif stage == "turn1":
                    n = TILE[i][1]
                    if i == 0:
                        pe.wait_ge(small_in, 16)
                    pe.wait_ge(xn_ready[0], i + 1)
                    b = take_bank(stage, i)
                    for c in range(DC):
                        ins = nc.tensor.transpose(b[:, c * P:c * P + n], xn[0:n, 0, i, c * P:(c + 1) * P],
                                                  ident[0:n, 0:n])
                    ins.then_inc(xn1_turned, 1)
                elif stage == "qk":
                    t0, n = TILE[i]
                    pe.wait_ge(xn1_t_ready, i + 1)
                    b = take_bank(stage, i)
                    for m in range(2):
                        for c in range(DC):
                            ins = nc.tensor.matmul(b[:, m * P:m * P + n], wqkv[:, c, m, :],
                                                   xn1_t[:, c, t0:t0 + n], start=c == 0, stop=c == DC - 1)
                    ins.then_inc(qk_done, 1)
                elif stage == "v":
                    t0, n = SPAN[i]
                    pe.wait_ge(xn1_t_ready, (t0 + n - 1) // P + 1)
                    b = take_bank(stage, i)
                    for c in range(DC):
                        ins = nc.tensor.matmul(b[0:n, 0:HEAD], xn1_t[:, c, t0:t0 + n], wqkv[:, c, 2, :],
                                               start=c == 0, stop=c == DC - 1)
                    ins.then_inc(v_done, 1)
                elif stage == "scores":
                    t0, n = SPAN[i]
                    pe.wait_ge(qk_ready, 2 * ((t0 + n - 1) // P + 1))
                    nc.tensor.matmul(take_bank(stage, i)[0:n, 0:n], q_t[:, t0:t0 + n], k_t[:, t0:t0 + n],
                                     start=True, stop=True).then_inc(scores_done, 1)
                elif stage == "turnp":
                    n = SPAN[i][1]
                    pe.wait_ge(probs_n_ready, i + 1)
                    nc.tensor.transpose(take_bank(stage, i)[0:n, 0:n], probs_n[0:n, i, 0:n],
                                        ident[0:n, 0:n]).then_inc(probs_turned, 1)
                elif stage == "pv":
                    n = SPAN[i][1]
                    pe.wait_ge(probs_t_ready, i + 1)
                    pe.wait_ge(v_ready, i + 1)
                    nc.tensor.matmul(take_bank(stage, i)[:, 0:n], v[0:n, i, :], probs_t[0:n, i, 0:n],
                                     start=True, stop=True).then_inc(pv_done, 1)
                elif stage == "project":
                    t0, n = TILE[i]
                    if i == 0:
                        pe.wait_ge(ones_ready, 1)
                        pe.wait_ge(bias_tables_ready, 1)
                    pe.wait_ge(o_t_ready, (t0 + n - 1) // GROUP + 1)
                    b = take_bank(stage, i)[0:n, 0:D]
                    nc.tensor.matmul(b, o_t[:, t0:t0 + n], col("wo"), start=True, stop=False)
                    nc.tensor.matmul(b, ones[0:BO_ROWS, 0:n], bo[0:BO_ROWS, :], start=False,
                                     stop=True).then_inc(projected, 1)
                elif stage == "turn2":
                    n = TILE[i][1]
                    pe.wait_ge(xn_ready[1], i + 1)
                    b = take_bank(stage, i)
                    for c in range(DC):
                        ins = nc.tensor.transpose(b[:, c * P:c * P + n], xn[0:n, 1, i, c * P:(c + 1) * P],
                                                  ident[0:n, 0:n])
                    ins.then_inc(xn2_turned, 1)
                elif stage == "gate":
                    n = TILE[i][1]
                    pe.wait_ge(xn2_t_ready, 2 * (i + 1))
                    b = take_bank(stage, i)
                    for c in range(DC):
                        ins = nc.tensor.matmul(b[0:n, 0:EXPERTS], xn2_t[:, i, c, 0:n], gate_w[:, c, :],
                                               start=c == 0, stop=c == DC - 1)
                    ins.then_inc(gate_done, 1)
                elif stage == "turnw":
                    n = TILE[i][1]
                    pe.wait_ge(w_stack_ready, 3 * (i + 1))
                    nc.tensor.transpose(take_bank(stage, i)[0:EB_ROWS, 0:n], w_stack[0:n, i, :].bitcast(F32),
                                        ident[0:n, 0:n]).then_inc(weights_turned, 1)
                elif stage == "bias":
                    n = TILE[i][1]
                    if i == 0:
                        pe.wait_ge(bias_tables_ready, 2)
                    pe.wait_ge(w_stack_t_ready, i + 1)
                    nc.tensor.matmul(take_bank(stage, i)[0:n, 0:D], w_stack_t[0:EB_ROWS, i, 0:n], eb[0:EB_ROWS, :],
                                     start=True, stop=True).then_inc(biased, 1)
                elif stage == "expert":
                    t, q = divmod(i, QUARTERS)
                    n = TILE[t][1]
                    bank = y_bank[i % Y_BANKS][0:n, :]
                    if i >= Y_BANKS:
                        last_t, last_q = divmod(i - Y_BANKS, QUARTERS)
                        if last_q == 0:
                            pe.wait_ge(y_scaled, PER_QUARTER * (last_t + 1))
                        else:
                            pe.wait_ge(y_added, (QUARTERS - 1) * last_t + last_q)
                    pe.wait_ge(xn2_lo_ready, t + 1)
                    for c in range(DC):
                        w = DC * q + c
                        if t == 0:
                            pe.wait_ge(ew_lo_ready[EW_LOW[w]], count_of(EW_LOW, EW_LOW[w], w))
                        ins = three(bank, xn2_hi[:, t, c, 0:n], xn2_lo[:, t, c, 0:n], ew_hi[:, w, :], ew_lo[:, w, :],
                                    c == 0, c == DC - 1)
                    ins.then_inc(y_done, 1)


def kernel(**inputs):
    import numpy as np
    import concourse.bacc as bacc
    from concourse.bass_utils import run_bass_kernel_spmd

    a = {k: np.asarray(x) for k, x in inputs.items()}
    f32 = np.float32

    patches = a["x"].reshape(IMAGES, CHANNELS, GRID, PATCH, GRID, PATCH).transpose(1, 3, 5, 0, 2, 4)
    cols = np.zeros((F, IMAGES, SEQ), f32)
    cols[:, :, 2:] = patches.reshape(F, IMAGES, SEQ - 2)
    cols = cols.reshape(FC, P, TOKENS).transpose(1, 0, 2)
    x_t = np.concatenate([cols[:, :, t0:t0 + n].reshape(P, FC * n) for t0, n in TILE], axis=1)
    w_lin_t = a["L0_tok_W_lin"].T.reshape(FC, P, D).transpose(1, 0, 2)
    expert_w = a["L0_ffn_expert_w"].reshape(QUARTERS, PER_QUARTER, DC, P, D).transpose(3, 0, 2, 1, 4)

    first_small, small = np.zeros((TABLE_ROWS, FIRST_SMALL), f32), np.zeros((P, SMALL), f32)

    def put(name, block, row=0):
        block = block.reshape(block.shape[0], -1)
        to, at = (first_small, FIRST_COL) if name in FIRST_COL else (small, COL)
        to[row:row + block.shape[0], at[name][0]:at[name][1]] = block

    position = a["L0_tok_position_embeddings"][0]
    table_a = np.concatenate([a["cls_tok"][0], position])
    table_b = np.zeros((SEQ, D), f32)
    table_b[1] = a["L0_tok_class_token"][0, 0]
    table_b[2:] = a["L0_tok_b_lin"]
    onehot = np.tile(np.eye(SEQ, dtype=f32), (1, IMAGES))[:, 0:ONEHOT]
    for row in (0, TABLE_LO):
        put("table_a", table_a, row)
        put("table_b", table_b, row)
        put("onehot", onehot, row)
    put("ident", np.eye(P, dtype=f32))
    wqkv = np.stack([a["L0_attn_W" + m].T.reshape(DC, P, HEAD) for m in "qkv"])
    put("wqkv", wqkv.transpose(2, 1, 0, 3))
    put("biases", np.stack([a["L0_attn_b" + m] for m in "qkv"], axis=1))
    r = np.arange(GROUP)
    is_open = (r[:, None] // SEQ == r[None, :] // SEQ) & (r[:, None] >= r[None, :])
    put("mask", np.where(is_open, f32(0), f32(CLOSED)))
    put("wo", a["L0_attn_Wo"].T)
    for row in (0, 32):
        put("bo", a["L0_attn_bo"][None], row)
    put("gate_w", a["L0_ffn_gate_w"].reshape(DC, P, EXPERTS).transpose(1, 0, 2))
    put("gate_b", np.broadcast_to(a["L0_ffn_gate_b"], (P, EXPERTS)))
    for row in (0, 32, 64):
        put("expert_b", a["L0_ffn_expert_b"], row)

    arrays = {"x_t": x_t, "w_lin_t": w_lin_t, "first_small": first_small, "small": small,
              "expert_w": expert_w.reshape(P, QUARTERS * DC, BANK)}
    arrays = {k: np.ascontiguousarray(x) for k, x in arrays.items()}
    nc = bacc.Bacc("TRN2", target_bir_lowering=False, num_devices=1)
    args = [nc.dram_tensor(k, x.shape, F32, kind="ExternalInput").ap() for k, x in arrays.items()]
    args.append(nc.dram_tensor("out", (TOKENS, D), F32, kind="ExternalOutput").ap())
    build(nc, *args)
    res = run_bass_kernel_spmd(nc, [arrays], core_ids=[0])
    return res.results[0]["out"].reshape(IMAGES, SEQ, D)
```

```python
from contextlib import ExitStack

import concourse.bass as bass
from concourse import mybir

F32 = mybir.dt.float32
F32R = mybir.dt.float32r
ALU = mybir.AluOpType
ACT = mybir.ActivationFunctionType

P = 128
IMAGES, CHANNELS, SIDE, PATCH = 16, 3, 96, 16
GRID = SIDE // PATCH
SEQ = GRID * GRID + 2
TOKENS = IMAGES * SEQ
D = 256
DC = D // P
F = CHANNELS * PATCH * PATCH
FC = F // P
HEAD = 128
EXPERTS = 8
THRESHOLD = 0.1
EPS = 1e-5
SUM_GUARD = 0.5
TILES = -(-TOKENS // P)
IMAGES_PER_GROUP = P // SEQ
GROUP = IMAGES_PER_GROUP * SEQ
GROUPS = -(-TOKENS // GROUP)
BANK = 512
QUARTERS = EXPERTS * D // BANK
PER_QUARTER = EXPERTS // QUARTERS
MISC_BANKS, Y_BANKS = 5, 3
EMBED_STEPS = 3
EMBED_CHUNKS = FC // EMBED_STEPS
SCALAR_TILES = TILES - 1
LAST_QUARTER = TILES * QUARTERS - 1
CLOSED = -1.0e30

ADDED_ROWS = SEQ + 2
TABLE_LO = 64
TABLE_ROWS = TABLE_LO + ADDED_ROWS
EB_ROWS = 64 + EXPERTS

TILE = [(P * t, min(P, TOKENS - P * t)) for t in range(TILES)]
SPAN = [(GROUP * g, min(GROUP, TOKENS - GROUP * g)) for g in range(GROUPS)]

ONEHOT = SEQ + P


def _columns(*widths):
    at, n = {}, 0
    for name, width in widths:
        at[name] = (n, n + width)
        n += width
    return at, n


FIRST_COL, FIRST_SMALL = _columns(("table", D), ("onehot", ONEHOT))
COL, SMALL = _columns(("ident", P), ("wqkv", DC * 3 * HEAD), ("biases", 3), ("mask", GROUP), ("gate_w", DC * EXPERTS),
                      ("gate_b", EXPERTS), ("wo", D), ("bo", D))
BIAS_COL, BIAS_SMALL = _columns(("expert_b", D))


def _cut(*sizes):
    return [(sum(sizes[:i]), size) for i, size in enumerate(sizes)]


X_CUTS = [[], _cut(2, 2, 2), _cut(2, 2, 2), _cut(3, 3), _cut(3, 3)]
PIECES = [(t, c, chunks) for t in range(TILES) for c, chunks in X_CUTS[t]]
WL_PIECES = _cut(1, 1, 2, 2)
WL_WIDE = D + P

ORDER = {
    "sync": (
        "load_wl.0 load_wl.1 load_wl.2 load_wl.3 load_x.0 load_table.0 load_x.1 load_x.2 load_x.3 "
        "load_x.4 load_x.5 load_small.0 load_x.6 load_x.7 load_biases.0 load_ew.0 load_x.8 load_ew.1 "
        "load_ew.2 load_x.9 load_ew.3"),
    "tensor": (
        "warm_up.0 warm_up.1 warm_up.2 warm_up.3 warm_up.4 warm_up.5 warm_up.6 warm_up.7 warm_up.8 "
        "embed_hi.0 warm_up.9 warm_up.10 warm_up.11 warm_up.12 embed_lo.0 embed_hi.1 warm_up.13 "
        "embed_lo.1 embed_hi.2 embed_hi.3 embed_lo.2 embed_lo.3 embed_hi.4 embed_hi.5 embed_lo.4 "
        "warm_up.14 embed_lo.5 warm_up.15 turn1.0 embed_hi.6 embed_hi.7 embed_lo.6 qk.0 embed_lo.7 "
        "embed_hi.8 embed_lo.8 embed_hi.9 embed_lo.9 scores.0 turn1.1 embed_hi.10 embed_hi.11 "
        "embed_lo.10 embed_lo.11 v.0 qk.1 v.1 embed_hi.12 turn1.2 embed_lo.12 embed_hi.13 embed_hi.14 "
        "embed_lo.13 embed_lo.14 qk.2 turn1.3 scores.1 v.2 scores.2 qk.3 turnp.0 turnp.1 v.3 turn1.4 "
        "scores.3 pv.0 pv.1 qk.4 project.0 turnp.2 scores.4 turnp.3 pv.2 scores.5 pv.3 v.4 project.1 "
        "turn2.0 v.5 turnp.4 project.2 gate.0 pv.4 expert.0 expert.1 turnp.5 turn2.1 project.3 expert.2 "
        "pv.5 expert.3 project.4 expert.4 turnw.0 gate.1 turn2.2 expert.5 bias.0 expert.6 turn2.3 "
        "expert.7 gate.2 expert.8 expert.9 gate.3 turnw.1 expert.10 turn2.4 expert.11 expert.12 bias.1 "
        "expert.13 gate.4 turnw.2 expert.14 expert.15 turnw.3 expert.16 expert.17 expert.18 bias.2 "
        "expert.19 expert.20 expert.21 expert.22 expert.23 expert.24 expert.25 turnw.4 expert.26 "
        "expert.27 expert.28 bias.3 expert.29 bias.4 expert.30 expert.31 expert.32 expert.33 expert.34 "
        "expert.35 expert.36 expert.37 expert.38 expert.39"),
    "scalar": (
        "wl_hi.3 onehot.0 x_hi.0 x_hi.2 x_hi.3 copy_h.0 x_hi.4 copy_x1.0 copy_h.1 copy_qk.0 copy_h.2 "
        "x_hi.8 copy_x1.1 copy_h.3 copy_v.0 exp.0 copy_v.1 copy_x1.2 bias_hi.0 ew_hi.3 copy_qk.1 ew_hi.7 "
        "copy_h.4 copy_qk.2 copy_x1.3 copy_v.2 exp.1 exp.2 copy_qk.3 copy_p.0 copy_p.1 copy_v.3 "
        "copy_x1.4 copy_o.0 copy_o.1 exp.3 copy_qk.4 copy_p.2 copy_p.3 copy_o.2 exp.4 copy_o.3 copy_v.4 "
        "copy_x2.0 copy_p.4 exp.5 copy_v.5 copy_o.4 copy_p.5 gate_exp.0 copy_o.5 copy_x2.1 scale_y.0 "
        "copy_w.0 gate_exp.1 copy_x2.2 copy_x2.3 gate_exp.2 gate_exp.3 copy_w.1 scale_y.1 copy_x2.4 "
        "copy_w.2 gate_exp.4 scale_y.2 copy_w.3 copy_w.4 scale_y.3"),
    "vector": (
        "wl_hi.0 wl_hi.1 wl_hi.2 wl_lo.2 wl_lo.3 table.0 x_hi.1 stats1.0 x_hi.5 x_lo.2 x_lo.3 norm1.0 "
        "x_hi.6 x_lo.4 stats1.1 x_lo.5 x_lo.6 norm1.1 stats1.2 x_lo.7 max.0 ew_hi.0 ew_hi.1 stats1.3 "
        "x_hi.9 norm1.2 norm_p.0 norm1.3 ew_hi.2 stats1.4 max.1 ew_lo.0 max.2 norm_p.1 ew_hi.4 norm1.4 "
        "bias_lo.0 norm_p.2 ew_hi.5 ew_hi.6 max.3 norm_p.3 stats2.0 max.4 ew_lo.7 max.5 norm2.0 norm_p.4 "
        "stats2.1 x2_lo.0 norm_p.5 logits.0 norm2.1 stats2.2 pick.0 stats2.3 norm2.2 stats2.4 norm2.3 "
        "logits.1 x2_lo.1 pick.1 start_acc.0 add_y.1 logits.2 add_y.2 pick.2 norm2.4 add_y.3 logits.3 "
        "pick.3 start_acc.1 x2_lo.2 add_y.5 add_y.6 x2_lo.3 add_y.7 logits.4 pick.4 start_acc.2 add_y.9 "
        "x2_lo.4 add_y.10 add_y.11 start_acc.3 add_y.13 add_y.14 add_y.15 start_acc.4 add_y.16 add_y.17 "
        "add_y.18 add_y.19"),
    "gpsimd": (
        "wl_lo.0 wl_lo.1 x_lo.0 x_lo.1 rstd1.0 rstd1.1 x_hi.7 rstd1.2 add_bo.0 x_lo.8 add_bo.1 rstd1.3 "
        "x_lo.9 add_bo.2 add_bo.3 ew_lo.1 rstd1.4 ew_lo.2 ew_lo.3 ew_lo.4 rstd2.0 add_bo.4 ew_lo.5 "
        "rstd2.1 ew_lo.6 rstd2.2 weights.0 rstd2.3 add_hidden.0 rstd2.4 weights.1 weights.2 add_hidden.1 "
        "weights.3 finish.0 add_hidden.2 finish.1 weights.4 add_hidden.3 finish.2 finish.3"),
}

ITEMS = {"wl_hi": len(WL_PIECES), "wl_lo": len(WL_PIECES), "x_hi": len(PIECES), "x_lo": len(PIECES),
         "ew_hi": QUARTERS * DC, "ew_lo": QUARTERS * DC}
OWNER = {stage: [next(e for e in ORDER if f"{stage}.{i}" in ORDER[e].split()) for i in range(items)]
         for stage, items in ITEMS.items()}


def steps_of(engine):
    for word in ORDER[engine].split():
        stage, index = word.split(".")
        yield stage, int(index)


MISC_USE = {step: use for use, step in enumerate(
    ("embed", i // EMBED_STEPS) if stage == "embed_hi" else (stage, i) for stage, i in steps_of("tensor")
    if stage not in ("warm_up", "expert", "embed_lo") and (stage != "embed_hi" or i % EMBED_STEPS == 0))}


def added_by(i):
    return PER_QUARTER * (i + 1 - min(i // QUARTERS + 1, SCALAR_TILES))


def count_of(stage, i):
    return OWNER[stage][0:i + 1].count(OWNER[stage][i])


def build(nc, x_t, w_and_x_t, first_small, small, bias_small, expert_w, out):
    ctx = ExitStack()
    with ctx:
        def sb(name, shape, dt=F32):
            return ctx.enter_context(nc.sbuf_tensor(name, shape, dt))

        def psum(name):
            return ctx.enter_context(nc.psum_tensor(name, [P, BANK], F32))

        def sem(name):
            return ctx.enter_context(nc.semaphore(name))

        x_raw = sb("x_raw", [P, FC * (TOKENS - P)])
        x_hi = sb("x_hi", [P, FC * (TOKENS - P)], F32R)
        x_lo = sb("x_lo", [P, FC * (TOKENS - P)], F32R)
        wl_raw = sb("wl_raw", [P, FC, WL_WIDE])
        wl_hi = sb("wl_hi", [P, FC, WL_WIDE], F32R)
        wl_lo = sb("wl_lo", [P, FC, WL_WIDE], F32R)
        ew_raw = sb("ew_raw", [P, QUARTERS * DC, BANK])
        ew_hi = sb("ew_hi", [P, QUARTERS * DC, BANK], F32R)
        ew_lo = sb("ew_lo", [P, QUARTERS * DC, BANK], F32R)
        first_sm = sb("first_sm", [P, FIRST_SMALL])
        sm = sb("sm", [P, SMALL])
        bias_sm = sb("bias_sm", [P, BIAS_SMALL])
        table = sb("table", [P, D], F32R)
        onehot = sb("onehot", [P, ONEHOT], F32R)
        ones = sb("ones", [P, D], F32R)
        eb = sb("eb", [P, D], F32R)
        hidden = sb("hidden", [P, 2, TILES, D])
        stats = sb("stats", [P, 2, TILES, 6])
        moments = sb("moments", [P, 2, TILES, 2])
        var_eps = sb("var_eps", [P, 2, TILES, 1])
        minus_half = sb("minus_half", [P, 1])
        minus_one = sb("minus_one", [P, 1])
        rstd = sb("rstd", [P, 2, TILES, 1])
        xn = sb("xn", [P, 2, TILES, D])
        xn1_t = sb("xn1_t", [P, DC, TOKENS])
        q_t = sb("q_t", [P, TOKENS])
        k_t = sb("k_t", [P, TOKENS])
        v = sb("v", [P, GROUPS, HEAD])
        scores = sb("scores", [P, GROUPS, GROUP])
        minus_max = sb("minus_max", [P, GROUPS])
        row_sum = sb("row_sum", [P, GROUPS])
        row_inv = sb("row_inv", [P, GROUPS])
        probs = sb("probs", [P, GROUPS, GROUP])
        probs_n = sb("probs_n", [P, GROUPS, GROUP])
        probs_t = sb("probs_t", [P, GROUPS, GROUP])
        o_t = sb("o_t", [P, TOKENS])
        xn2_t = sb("xn2_t", [P, TILES, DC, P])
        xn2_hi = sb("xn2_hi", [P, TILES, DC, P], F32R)
        xn2_lo = sb("xn2_lo", [P, TILES, DC, P], F32R)
        logits = sb("logits", [P, TILES, EXPERTS])
        gate_exp = sb("gate_exp", [P, TILES, EXPERTS])
        picked = sb("picked", [P, TILES, EXPERTS])
        weights = sb("weights", [P, TILES, EXPERTS])
        gate_cols = sb("gate_cols", [P, TILES, 6])
        w_stack = sb("w_stack", [P, TILES, EB_ROWS], F32R)
        w_stack_t = sb("w_stack_t", [P, TILES, P], F32R)
        scaled = sb("scaled", [P, SCALAR_TILES, PER_QUARTER, D])
        acc = sb("acc", [P, TILES, D])

        misc = [psum(f"misc{i}") for i in range(MISC_BANKS)]
        y_bank = [psum(f"y_bank{i}") for i in range(Y_BANKS)]

        def col(name, rows=P):
            return sm[0:rows, COL[name][0]:COL[name][1]]

        def first_col(name):
            return first_sm[0:TABLE_ROWS, FIRST_COL[name][0]:FIRST_COL[name][1]]

        ident = col("ident")
        wqkv = col("wqkv").rearrange("p (c m h) -> p c m h", c=DC, m=3)
        gate_w = col("gate_w").rearrange("p (c e) -> p c e", c=DC)

        def x_of(buf, piece):
            t, c, chunks = PIECES[piece]
            at, n = FC * (TILE[t][0] - P) + c * TILE[t][1], TILE[t][1]
            return buf[:, at:at + chunks * n]

        def wl_of(buf, piece):
            c, chunks = WL_PIECES[piece]
            return buf[:, c:c + chunks, :]

        def ew_of(buf, chunk):
            return buf[:, chunk, :]

        def bias_col(name, rows):
            return bias_sm[rows, BIAS_COL[name][0]:BIAS_COL[name][1]]

        def bank_of(stage, i):
            return misc[MISC_USE[(stage, i)] % MISC_BANKS]

        wl_in = [sem(f"wl_in{i}") for i in range(len(WL_PIECES))]
        x_in = [sem(f"x_in{i}") for i in range(len(PIECES))]
        table_in, small_in, biases_in = sem("table_in"), sem("small_in"), sem("biases_in")
        ew_in = [sem(f"ew_in{q}") for q in range(QUARTERS)]
        out_stored = sem("out_stored")
        part_ready = {(stage, e): sem(f"{stage}_{e}") for stage in ITEMS for e in sorted(set(OWNER[stage]))}
        table_ready, onehot_ready, ones_ready = sem("table_ready"), sem("onehot_ready"), sem("ones_ready")
        bias_hi_ready = sem("bias_hi_ready")
        bias_lo_ready, stack_cleared, exponents_ready = sem("bias_lo_ready"), sem("stack_cleared"), sem("exponents_ready")
        dve_step, pool_step = sem("dve_step"), sem("pool_step")
        hidden_bo_ready = sem("hidden_bo_ready")
        embedded, h_ready, projected, h2_ready = sem("embedded"), sem("h_ready"), sem("projected"), sem("h2_ready")
        stats_ready = [sem("stats1_ready"), sem("stats2_ready")]
        var_ready = [sem("var1_ready"), sem("var2_ready")]
        rstd_ready = [sem("rstd1_ready"), sem("rstd2_ready")]
        xn_ready = [sem("xn1_ready"), sem("xn2_ready")]
        xn1_turned, xn1_t_ready = sem("xn1_turned"), sem("xn1_t_ready")
        qk_done, qk_ready, v_done, v_ready = sem("qk_done"), sem("qk_ready"), sem("v_done"), sem("v_ready")
        scores_done, scores_ready = sem("scores_done"), sem("scores_ready")
        probs_ready, probs_n_ready = sem("probs_ready"), sem("probs_n_ready")
        probs_turned, probs_t_ready = sem("probs_turned"), sem("probs_t_ready")
        pv_done, o_t_ready = sem("pv_done"), sem("o_t_ready")
        xn2_turned, xn2_t_ready, xn2_lo_ready = sem("xn2_turned"), sem("xn2_t_ready"), sem("xn2_lo_ready")
        gate_done, logits_ready = sem("gate_done"), sem("logits_ready")
        gate_exp_ready = sem("gate_exp_ready")
        limit_ready, picked_ready = sem("limit_ready"), sem("picked_ready")
        weights_ready, w_stack_ready = sem("weights_ready"), sem("w_stack_ready")
        weights_turned, w_stack_t_ready = sem("weights_turned"), sem("w_stack_t_ready")
        biased, acc_ready = sem("biased"), sem("acc_ready")
        y_done, y_scaled, start_ready = sem("y_done"), sem("y_scaled"), sem("start_ready")
        y_added, finished = sem("y_added"), sem("finished")

        split_of = {"wl": (wl_of, wl_raw, wl_hi, wl_lo), "x": (x_of, x_raw, x_hi, x_lo),
                    "ew": (ew_of, ew_raw, ew_hi, ew_lo)}

        def wait_loaded(engine, operand, i):
            engine.wait_ge({"wl": wl_in[i:], "x": x_in[i:], "ew": ew_in[i // DC:]}[operand][0], 16)

        def wait_part(engine, stage, i):
            engine.wait_ge(part_ready[(stage, OWNER[stage][i])], count_of(stage, i))

        last_reader = {"embed": (h_ready, 1), "turn1": (xn1_t_ready, 1), "qk": (qk_ready, 2), "v": (v_ready, 1),
                       "scores": (scores_ready, 1), "turnp": (probs_t_ready, 1), "pv": (o_t_ready, 1),
                       "project": (h2_ready, 1), "turn2": (xn2_t_ready, 2), "gate": (logits_ready, 1),
                       "turnw": (w_stack_t_ready, 1), "bias": (acc_ready, 1)}

        block = ctx.enter_context(nc.Block())

        @block.sync
        def _(sp):
            for stage, i in steps_of("sync"):
                if stage == "load_wl":
                    sp.dma_start(wl_of(wl_raw, i), wl_of(w_and_x_t, i)).then_inc(wl_in[i], 16)
                elif stage == "load_x":
                    sp.dma_start(x_of(x_raw, i), x_of(x_t, i)).then_inc(x_in[i], 16)
                elif stage == "load_ew":
                    c = slice(DC * i, DC * (i + 1))
                    sp.dma_start(ew_raw[:, c, :], expert_w[:, c, :]).then_inc(ew_in[i], 16)
                elif stage == "load_table":
                    sp.dma_start(first_sm[0:TABLE_ROWS, :], first_small).then_inc(table_in, 16)
                elif stage == "load_small":
                    sp.dma_start(sm[:], small).then_inc(small_in, 16)
                elif stage == "load_biases":
                    sp.dma_start(bias_sm[0:EB_ROWS, :], bias_small).then_inc(biases_in, 16)
            for t in range(TILES):
                t0, n = TILE[t]
                if t < SCALAR_TILES:
                    sp.wait_ge(finished, t + 1)
                else:
                    sp.wait_ge(y_added, added_by(QUARTERS * (t + 1) - 1))
                sp.dma_start(out[t0:t0 + n, :], acc[0:n, t, :]).then_inc(out_stored, 16)
            sp.wait_ge(out_stored, 16 * TILES)

        @block.gpsimd
        def _(pool):
            nc.gpsimd.memset(minus_half[:], -0.5).then_inc(exponents_ready, 1)
            nc.gpsimd.memset(minus_one[:], -1.0).then_inc(exponents_ready, 1)
            pool.wait_ge(exponents_ready, 2)

            steps = [0]

            def then(ins):
                steps[0] += 1
                ins.then_inc(pool_step, 1)
                pool.wait_ge(pool_step, steps[0])

            pool.wait_ge(stack_cleared, 1)
            for stage, i in steps_of("gpsimd"):
                if stage in ("wl_hi", "x_hi", "ew_hi"):
                    of, raw, hi, lo = split_of[stage[:-3]]
                    wait_loaded(pool, stage[:-3], i)
                    nc.gpsimd.tensor_copy(of(hi, i), of(raw, i)).then_inc(part_ready[(stage, "gpsimd")], 1)
                elif stage in ("wl_lo", "x_lo", "ew_lo"):
                    of, raw, hi, lo = split_of[stage[:-3]]
                    wait_part(pool, stage[:-3] + "_hi", i)
                    nc.gpsimd.tensor_tensor(of(lo, i), of(raw, i), of(hi, i).bitcast(F32),
                                            ALU.subtract).then_inc(part_ready[(stage, "gpsimd")], 1)
                elif stage == "add_bo":
                    n = TILE[i][1]
                    if i == 0:
                        pool.wait_ge(small_in, 16)
                    pool.wait_ge(xn_ready[0], i + 1)
                    nc.gpsimd.tensor_tensor(hidden[0:n, 0, i, :], hidden[0:n, 0, i, :], col("bo", n),
                                            ALU.add).then_inc(hidden_bo_ready, 1)
                elif stage in ("rstd1", "rstd2"):
                    which, n = int(stage[-1]) - 1, TILE[i][1]
                    pool.wait_ge(var_ready[which], i + 1)
                    then(nc.gpsimd.tensor_scalar(var_eps[0:n, which, i, :], moments[0:n, which, i, 1:2], EPS, None,
                                                 ALU.add))
                    nc.gpsimd.tensor_tensor(rstd[0:n, which, i, :], var_eps[0:n, which, i, :], minus_half[0:n, :],
                                            ALU.pow).then_inc(rstd_ready[which], 1)
                elif stage == "weights":
                    n = TILE[i][1]
                    c = gate_cols[0:n, i, :]
                    pool.wait_ge(picked_ready, i + 1)
                    then(nc.gpsimd.tensor_scalar(c[:, 4:5], c[:, 3:4], SUM_GUARD, None, ALU.max))
                    then(nc.gpsimd.tensor_tensor(c[:, 5:6], c[:, 4:5], minus_one[0:n, :], ALU.pow))
                    nc.gpsimd.tensor_scalar(weights[0:n, i, :], picked[0:n, i, :], c[:, 5:6], None,
                                            ALU.mult).then_inc(weights_ready, 1)
                    nc.gpsimd.tensor_scalar(w_stack[0:n, i, 0:EXPERTS], picked[0:n, i, :], c[:, 5:6], None,
                                            ALU.mult).then_inc(w_stack_ready, 1)
                    nc.gpsimd.tensor_scalar(w_stack[0:n, i, 32:32 + EXPERTS], picked[0:n, i, :], c[:, 5:6], None,
                                            ALU.mult).then_inc(w_stack_ready, 1)
                    pool.wait_ge(weights_ready, i + 1)
                    pool.wait_ge(w_stack_ready, 3 * i + 1)
                    nc.gpsimd.tensor_tensor(w_stack[0:n, i, 64:64 + EXPERTS], weights[0:n, i, :],
                                            w_stack[0:n, i, 0:EXPERTS].bitcast(F32),
                                            ALU.subtract).then_inc(w_stack_ready, 1)
                elif stage == "add_hidden":
                    n = TILE[i][1]
                    pool.wait_ge(y_scaled, PER_QUARTER * i + 1)
                    pool.wait_ge(h2_ready, i + 1)
                    nc.gpsimd.tensor_tensor(scaled[0:n, i, 0, :], scaled[0:n, i, 0, :], hidden[0:n, 1, i, :],
                                            ALU.add).then_inc(start_ready, 1)
                elif stage == "finish":
                    n = TILE[i][1]
                    pool.wait_ge(y_added, added_by(QUARTERS * (i + 1) - 1))
                    nc.gpsimd.tensor_tensor(acc[0:n, i, :], acc[0:n, i, :], scaled[0:n, i, 1, :],
                                            ALU.add).then_inc(finished, 1)

        @block.scalar
        def _(act):
            for stage, i in steps_of("scalar"):
                if stage in ("wl_hi", "x_hi", "ew_hi"):
                    of, raw, hi, lo = split_of[stage[:-3]]
                    wait_loaded(act, stage[:-3], i)
                    nc.scalar.copy(of(hi, i), of(raw, i)).then_inc(part_ready[(stage, "scalar")], 1)
                elif stage == "onehot":
                    act.wait_ge(table_in, 16)
                    nc.scalar.copy(onehot[0:TABLE_ROWS, :], first_col("onehot")).then_inc(onehot_ready, 1)
                elif stage == "bias_hi":
                    act.wait_ge(biases_in, 16)
                    nc.scalar.copy(eb[0:EB_ROWS, :], bias_col("expert_b", slice(0, EB_ROWS))).then_inc(bias_hi_ready, 1)
                elif stage == "copy_h":
                    n = TILE[i][1]
                    act.wait_ge(stats_ready[0], i + 1)
                    nc.scalar.copy(hidden[0:n, 0, i, :], bank_of("embed", i)[0:n, 0:D]).then_inc(h_ready, 1)
                elif stage == "copy_x1":
                    t0, n = TILE[i]
                    act.wait_ge(xn1_turned, i + 1)
                    nc.scalar.copy(xn1_t[:, :, t0:t0 + n],
                                   bank_of("turn1", i)[:, 0:D].rearrange("p (c n) -> p c n", c=DC)[:, :, 0:n]
                                   ).then_inc(xn1_t_ready, 1)
                elif stage == "copy_qk":
                    t0, n = TILE[i]
                    if i == 0:
                        act.wait_ge(small_in, 16)
                    act.wait_ge(qk_done, i + 1)
                    for m, to in enumerate((q_t, k_t)):
                        nc.scalar.activation(to[:, t0:t0 + n], bank_of("qk", i)[:, m * P:m * P + n], ACT.Identity,
                                             bias=col("biases")[:, m:m + 1]).then_inc(qk_ready, 1)
                elif stage == "copy_v":
                    n = SPAN[i][1]
                    act.wait_ge(v_done, i + 1)
                    nc.scalar.copy(v[0:n, i, :], bank_of("v", i)[0:n, 0:HEAD]).then_inc(v_ready, 1)
                elif stage == "exp":
                    n = SPAN[i][1]
                    act.wait_ge(scores_ready, i + 1)
                    nc.scalar.activation(probs[0:n, i, 0:n], scores[0:n, i, 0:n], ACT.Exp,
                                         bias=minus_max[0:n, i:i + 1], scale=-1.0,
                                         accum_out=row_sum[0:n, i:i + 1]).then_inc(probs_ready, 1)
                elif stage == "copy_p":
                    n = SPAN[i][1]
                    act.wait_ge(probs_turned, i + 1)
                    nc.scalar.copy(probs_t[0:n, i, 0:n], bank_of("turnp", i)[0:n, 0:n]).then_inc(probs_t_ready, 1)
                elif stage == "copy_o":
                    t0, n = SPAN[i]
                    act.wait_ge(pv_done, i + 1)
                    nc.scalar.activation(o_t[:, t0:t0 + n], bank_of("pv", i)[:, 0:n], ACT.Identity,
                                         bias=col("biases")[:, 2:3]).then_inc(o_t_ready, 1)
                elif stage == "copy_x2":
                    n = TILE[i][1]
                    act.wait_ge(xn2_turned, i + 1)
                    src = bank_of("turn2", i)[:, 0:D].rearrange("p (c n) -> p c n", c=DC)[:, :, 0:n]
                    for to in (xn2_hi, xn2_t):
                        nc.scalar.copy(to[:, i, :, 0:n], src).then_inc(xn2_t_ready, 1)
                elif stage == "gate_exp":
                    n = TILE[i][1]
                    act.wait_ge(logits_ready, i + 1)
                    nc.scalar.activation(gate_exp[0:n, i, :], logits[0:n, i, :], ACT.Exp,
                                         bias=gate_cols[0:n, i, 0:1], scale=-1.0,
                                         accum_out=gate_cols[0:n, i, 1:2]).then_inc(gate_exp_ready, 1)
                    act.wait_ge(gate_exp_ready, i + 1)
                    nc.scalar.activation(gate_cols[0:n, i, 2:3], gate_cols[0:n, i, 1:2], ACT.Copy,
                                         scale=THRESHOLD).then_inc(limit_ready, 1)
                elif stage == "copy_w":
                    n = TILE[i][1]
                    act.wait_ge(weights_turned, i + 1)
                    nc.scalar.copy(w_stack_t[0:EB_ROWS, i, 0:n],
                                   bank_of("turnw", i)[0:EB_ROWS, 0:n]).then_inc(w_stack_t_ready, 1)
                elif stage == "scale_y":
                    n, y = TILE[i][1], QUARTERS * i
                    act.wait_ge(weights_ready, i + 1)
                    act.wait_ge(y_done, y + 1)
                    for e in range(PER_QUARTER):
                        nc.scalar.activation(scaled[0:n, i, e, :], y_bank[y % Y_BANKS][0:n, e * D:(e + 1) * D],
                                             ACT.Copy, scale=weights[0:n, i, e:e + 1]).then_inc(y_scaled, 1)

        @block.vector
        def _(dve):
            steps = [0]

            def then(ins):
                steps[0] += 1
                ins.then_inc(dve_step, 1)
                dve.wait_ge(dve_step, steps[0])

            def low(out_ap, raw, hi):
                return nc.vector.tensor_tensor(out_ap, raw, hi.bitcast(F32), ALU.subtract)

            def norm_stats(which, t, rows):
                n = TILE[t][1]
                nc.vector.bn_stats(stats[0:n, which, t, :], rows).then_inc(stats_ready[which], 1)
                dve.wait_ge(stats_ready[which], t + 1)
                nc.vector.bn_aggr(moments[0:n, which, t, :], stats[0:n, which, t, :]).then_inc(var_ready[which], 1)

            nc.vector.memset(ones[:].bitcast(F32), 1.0).then_inc(ones_ready, 1)
            nc.vector.memset(w_stack[:].bitcast(F32), 0.0).then_inc(stack_cleared, 1)

            for stage, i in steps_of("vector"):
                if stage in ("wl_hi", "x_hi", "ew_hi"):
                    of, raw, hi, lo = split_of[stage[:-3]]
                    wait_loaded(dve, stage[:-3], i)
                    nc.vector.tensor_copy(of(hi, i), of(raw, i)).then_inc(part_ready[(stage, "vector")], 1)
                elif stage in ("wl_lo", "x_lo", "ew_lo"):
                    of, raw, hi, lo = split_of[stage[:-3]]
                    wait_part(dve, stage[:-3] + "_hi", i)
                    low(of(lo, i), of(raw, i), of(hi, i)).then_inc(part_ready[(stage, "vector")], 1)
                elif stage == "table":
                    dve.wait_ge(table_in, 16)
                    then(nc.vector.tensor_copy(table[0:TABLE_ROWS, :], first_col("table")))
                    rows = slice(TABLE_LO, TABLE_ROWS)
                    low(table[rows, :], first_col("table")[rows, :], table[rows, :]).then_inc(table_ready, 1)
                elif stage == "bias_lo":
                    rows = slice(32, 32 + EXPERTS)
                    dve.wait_ge(bias_hi_ready, 1)
                    low(eb[rows, :], bias_col("expert_b", rows), eb[rows, :]).then_inc(bias_lo_ready, 1)
                elif stage == "stats1":
                    dve.wait_ge(embedded, i + 1)
                    norm_stats(0, i, bank_of("embed", i)[0:TILE[i][1], 0:D])
                elif stage in ("norm1", "norm2"):
                    which, n = int(stage[-1]) - 1, TILE[i][1]
                    dve.wait_ge(rstd_ready[which], i + 1)
                    if which == 0:
                        dve.wait_ge(h_ready, i + 1)
                    nc.vector.tensor_scalar(xn[0:n, which, i, :], hidden[0:n, which, i, :],
                                            moments[0:n, which, i, 0:1], rstd[0:n, which, i, :],
                                            ALU.subtract, ALU.mult).then_inc(xn_ready[which], 1)
                elif stage == "max":
                    n = SPAN[i][1]
                    dve.wait_ge(scores_done, i + 1)
                    nc.vector.tensor_tensor_reduce(out=scores[0:n, i, 0:n], in0=bank_of("scores", i)[0:n, 0:n],
                                                   in1=col("mask")[0:n, 0:n], scale=-float(HEAD) ** -0.5,
                                                   scalar=3.0e38, op0=ALU.add, op1=ALU.min,
                                                   accum_out=minus_max[0:n, i:i + 1]).then_inc(scores_ready, 1)
                elif stage == "norm_p":
                    n = SPAN[i][1]
                    dve.wait_ge(probs_ready, i + 1)
                    then(nc.vector.reciprocal(row_inv[0:n, i:i + 1], row_sum[0:n, i:i + 1]))
                    nc.vector.tensor_scalar(probs_n[0:n, i, 0:n], probs[0:n, i, 0:n], row_inv[0:n, i:i + 1], None,
                                            ALU.mult).then_inc(probs_n_ready, 1)
                elif stage == "stats2":
                    n = TILE[i][1]
                    dve.wait_ge(projected, i + 1)
                    dve.wait_ge(hidden_bo_ready, i + 1)
                    nc.vector.tensor_tensor(hidden[0:n, 1, i, :], bank_of("project", i)[0:n, 0:D],
                                            hidden[0:n, 0, i, :], ALU.add).then_inc(h2_ready, 1)
                    dve.wait_ge(h2_ready, i + 1)
                    norm_stats(1, i, hidden[0:n, 1, i, :])
                elif stage == "x2_lo":
                    n = TILE[i][1]
                    dve.wait_ge(xn2_t_ready, 2 * (i + 1))
                    low(xn2_lo[:, i, :, 0:n], xn2_t[:, i, :, 0:n], xn2_hi[:, i, :, 0:n]).then_inc(xn2_lo_ready, 1)
                elif stage == "logits":
                    n = TILE[i][1]
                    dve.wait_ge(gate_done, i + 1)
                    nc.vector.tensor_tensor_reduce(out=logits[0:n, i, :], in0=bank_of("gate", i)[0:n, 0:EXPERTS],
                                                   in1=col("gate_b")[0:n, :], scale=-1.0, scalar=3.0e38,
                                                   op0=ALU.add, op1=ALU.min,
                                                   accum_out=gate_cols[0:n, i, 0:1]).then_inc(logits_ready, 1)
                elif stage == "pick":
                    n = TILE[i][1]
                    dve.wait_ge(limit_ready, i + 1)
                    nc.vector.scalar_tensor_tensor(out=picked[0:n, i, :], in0=gate_exp[0:n, i, :],
                                                   scalar=gate_cols[0:n, i, 2:3], in1=gate_exp[0:n, i, :],
                                                   op0=ALU.is_ge, op1=ALU.mult,
                                                   accum_out=gate_cols[0:n, i, 3:4]).then_inc(picked_ready, 1)
                elif stage == "start_acc":
                    n = TILE[i][1]
                    dve.wait_ge(biased, i + 1)
                    if i < SCALAR_TILES:
                        dve.wait_ge(start_ready, i + 1)
                        rest = scaled[0:n, i, 0, :]
                    else:
                        rest = hidden[0:n, 1, i, :]
                    nc.vector.tensor_tensor(acc[0:n, i, :], bank_of("bias", i)[0:n, 0:D], rest,
                                            ALU.add).then_inc(acc_ready, 1)
                elif stage == "add_y":
                    t, q = divmod(i, QUARTERS)
                    n = TILE[t][1]
                    first = q == (1 if t < SCALAR_TILES else 0)
                    if first:
                        dve.wait_ge(weights_ready, t + 1)
                    dve.wait_ge(y_done, i + 1)
                    for j in range(PER_QUARTER):
                        e = PER_QUARTER * q + j
                        bank = y_bank[i % Y_BANKS]
                        if i == LAST_QUARTER and j > 0:
                            dve.wait_ge(y_done, i + 2)
                            bank = y_bank[(i + 1) % Y_BANKS]
                        total = acc[0:n, t, :] if t >= SCALAR_TILES or j == 0 else scaled[0:n, t, j, :]
                        if t >= SCALAR_TILES and (j > 0 or not first):
                            dve.wait_ge(y_added, added_by(i) - PER_QUARTER + j)
                        elif first and j == 0:
                            dve.wait_ge(acc_ready, t + 1)
                        elif first:
                            dve.wait_ge(y_scaled, PER_QUARTER * (t + 1))
                        else:
                            dve.wait_ge(y_added, added_by(i - 1) - PER_QUARTER + j + 1)
                        nc.vector.scalar_tensor_tensor(
                            out=total, in0=bank[0:n, j * D:(j + 1) * D], scalar=weights[0:n, t, e:e + 1], in1=total,
                            op0=ALU.mult, op1=ALU.add).then_inc(y_added, 1)

        @block.tensor
        def _(pe):
            misc_order = [None] * len(MISC_USE)
            for key, use in MISC_USE.items():
                misc_order[use] = key

            def take_bank(stage, i):
                use = MISC_USE[(stage, i)]
                if use >= MISC_BANKS:
                    last, j = misc_order[use - MISC_BANKS]
                    reader, count = last_reader[last]
                    pe.wait_ge(reader, count * (j + 1))
                return misc[use % MISC_BANKS]

            def three(out_ap, stat_hi, stat_lo, mov_hi, mov_lo, start, stop):
                nc.tensor.matmul(out_ap, stat_hi, mov_hi, start=start, stop=False)
                nc.tensor.matmul(out_ap, stat_hi, mov_lo, start=False, stop=False)
                return nc.tensor.matmul(out_ap, stat_lo, mov_hi, start=False, stop=stop)

            pe.wait_ge(ones_ready, 1)
            x_piece = {(t, c): i for i, (t, c, _) in enumerate(PIECES)}
            wl_piece = {c: i for i, (c, _) in enumerate(WL_PIECES)}
            for stage, i in steps_of("tensor"):
                if stage == "warm_up":
                    nc.tensor.matmul(y_bank[0][:, 0:D], ones[:, 0:P], ones[:, :], start=True, stop=True)
                elif stage in ("embed_hi", "embed_lo"):
                    t, step = divmod(i, EMBED_STEPS)
                    t0, n = TILE[t]
                    half = stage[-2:]
                    h = take_bank("embed", t) if (half, step) == ("hi", 0) else bank_of("embed", t)
                    h = h[0:n, 0:D]
                    if t == 0:
                        xh, xl = (b[:, :, D:WL_WIDE] for b in (wl_hi, wl_lo))
                    else:
                        xh, xl = (b[:, FC * (t0 - P):FC * (t0 - P + n)].rearrange("p (c n) -> p c n", c=FC)
                                  for b in (x_hi, x_lo))
                    for c in range(step * EMBED_CHUNKS, (step + 1) * EMBED_CHUNKS):
                        if (t, c) in x_piece:
                            wait_part(pe, "x_" + half, x_piece[(t, c)])
                        if t == 0 and c in wl_piece:
                            wait_part(pe, "wl_" + half, wl_piece[c])
                        if half == "hi":
                            nc.tensor.matmul(h, xh[:, c, :], wl_hi[:, c, 0:D], start=c == 0, stop=False)
                        else:
                            nc.tensor.matmul(h, xh[:, c, :], wl_lo[:, c, 0:D], start=False, stop=False)
                            nc.tensor.matmul(h, xl[:, c, :], wl_hi[:, c, 0:D], start=False, stop=False)
                    if (half, step) == ("lo", EMBED_STEPS - 1):
                        if t == 0:
                            pe.wait_ge(table_ready, 1)
                            pe.wait_ge(onehot_ready, 1)
                        nc.tensor.matmul(h, onehot[0:TABLE_ROWS, t0 % SEQ:t0 % SEQ + n], table[0:TABLE_ROWS, :],
                                         start=False, stop=True).then_inc(embedded, 1)
                elif stage == "turn1":
                    n = TILE[i][1]
                    if i == 0:
                        pe.wait_ge(small_in, 16)
                    pe.wait_ge(xn_ready[0], i + 1)
                    b = take_bank(stage, i)
                    for c in range(DC):
                        ins = nc.tensor.transpose(b[:, c * P:c * P + n], xn[0:n, 0, i, c * P:(c + 1) * P],
                                                  ident[0:n, 0:n])
                    ins.then_inc(xn1_turned, 1)
                elif stage == "qk":
                    t0, n = TILE[i]
                    pe.wait_ge(xn1_t_ready, i + 1)
                    b = take_bank(stage, i)
                    for m in range(2):
                        for c in range(DC):
                            ins = nc.tensor.matmul(b[:, m * P:m * P + n], wqkv[:, c, m, :],
                                                   xn1_t[:, c, t0:t0 + n], start=c == 0, stop=c == DC - 1)
                    ins.then_inc(qk_done, 1)
                elif stage == "v":
                    t0, n = SPAN[i]
                    pe.wait_ge(xn1_t_ready, (t0 + n - 1) // P + 1)
                    b = take_bank(stage, i)
                    for c in range(DC):
                        ins = nc.tensor.matmul(b[0:n, 0:HEAD], xn1_t[:, c, t0:t0 + n], wqkv[:, c, 2, :],
                                               start=c == 0, stop=c == DC - 1)
                    ins.then_inc(v_done, 1)
                elif stage == "scores":
                    t0, n = SPAN[i]
                    pe.wait_ge(qk_ready, 2 * ((t0 + n - 1) // P + 1))
                    nc.tensor.matmul(take_bank(stage, i)[0:n, 0:n], q_t[:, t0:t0 + n], k_t[:, t0:t0 + n],
                                     start=True, stop=True).then_inc(scores_done, 1)
                elif stage == "turnp":
                    n = SPAN[i][1]
                    pe.wait_ge(probs_n_ready, i + 1)
                    nc.tensor.transpose(take_bank(stage, i)[0:n, 0:n], probs_n[0:n, i, 0:n],
                                        ident[0:n, 0:n]).then_inc(probs_turned, 1)
                elif stage == "pv":
                    n = SPAN[i][1]
                    pe.wait_ge(probs_t_ready, i + 1)
                    pe.wait_ge(v_ready, i + 1)
                    nc.tensor.matmul(take_bank(stage, i)[:, 0:n], v[0:n, i, :], probs_t[0:n, i, 0:n],
                                     start=True, stop=True).then_inc(pv_done, 1)
                elif stage == "project":
                    t0, n = TILE[i]
                    pe.wait_ge(o_t_ready, (t0 + n - 1) // GROUP + 1)
                    b = take_bank(stage, i)[0:n, 0:D]
                    nc.tensor.matmul(b, o_t[:, t0:t0 + n], col("wo"), start=True, stop=True).then_inc(projected, 1)
                elif stage == "turn2":
                    n = TILE[i][1]
                    pe.wait_ge(xn_ready[1], i + 1)
                    b = take_bank(stage, i)
                    for c in range(DC):
                        ins = nc.tensor.transpose(b[:, c * P:c * P + n], xn[0:n, 1, i, c * P:(c + 1) * P],
                                                  ident[0:n, 0:n])
                    ins.then_inc(xn2_turned, 1)
                elif stage == "gate":
                    n = TILE[i][1]
                    pe.wait_ge(xn2_t_ready, 2 * (i + 1))
                    b = take_bank(stage, i)
                    for c in range(DC):
                        ins = nc.tensor.matmul(b[0:n, 0:EXPERTS], xn2_t[:, i, c, 0:n], gate_w[:, c, :],
                                               start=c == 0, stop=c == DC - 1)
                    ins.then_inc(gate_done, 1)
                elif stage == "turnw":
                    n = TILE[i][1]
                    pe.wait_ge(w_stack_ready, 3 * (i + 1))
                    nc.tensor.transpose(take_bank(stage, i)[0:EB_ROWS, 0:n], w_stack[0:n, i, :].bitcast(F32),
                                        ident[0:n, 0:n]).then_inc(weights_turned, 1)
                elif stage == "bias":
                    n = TILE[i][1]
                    if i == 0:
                        pe.wait_ge(bias_lo_ready, 1)
                    pe.wait_ge(w_stack_t_ready, i + 1)
                    nc.tensor.matmul(take_bank(stage, i)[0:n, 0:D], w_stack_t[0:EB_ROWS, i, 0:n], eb[0:EB_ROWS, :],
                                     start=True, stop=True).then_inc(biased, 1)
                elif stage == "expert":
                    y, half = divmod(i, 2)
                    t, q = divmod(y, QUARTERS)
                    n = TILE[t][1]
                    use = y + half if y == LAST_QUARTER else y
                    bank = y_bank[use % Y_BANKS][0:n, :]
                    if use >= Y_BANKS and (half == 0 or use > y):
                        last_t, last_q = divmod(use - Y_BANKS, QUARTERS)
                        if last_q == 0 and last_t < SCALAR_TILES:
                            pe.wait_ge(y_scaled, PER_QUARTER * (last_t + 1))
                        else:
                            pe.wait_ge(y_added, added_by(use - Y_BANKS))
                    pe.wait_ge(xn2_lo_ready, t + 1)
                    split = y == LAST_QUARTER
                    cols = slice(half * D, (half + 1) * D) if split else slice(0, BANK)
                    for c in range(DC) if split else (half,):
                        w = DC * q + c
                        if t == 0:
                            wait_part(pe, "ew_lo", w)
                        ins = three(bank[:, cols], xn2_hi[:, t, c, 0:n], xn2_lo[:, t, c, 0:n], ew_hi[:, w, cols],
                                    ew_lo[:, w, cols], c == 0, c == DC - 1)
                    if split or half == 1:
                        ins.then_inc(y_done, 1)


def kernel(**inputs):
    import numpy as np
    import concourse.bacc as bacc
    from concourse.bass_utils import run_bass_kernel_spmd

    a = {k: np.asarray(x) for k, x in inputs.items()}
    f32 = np.float32

    patches = a["x"].reshape(IMAGES, CHANNELS, GRID, PATCH, GRID, PATCH).transpose(1, 3, 5, 0, 2, 4)
    cols = np.zeros((F, IMAGES, SEQ), f32)
    cols[:, :, 2:] = patches.reshape(F, IMAGES, SEQ - 2)
    cols = cols.reshape(FC, P, TOKENS).transpose(1, 0, 2)
    x_t = np.concatenate([cols[:, :, t0:t0 + n].reshape(P, FC * n) for t0, n in TILE[1:]], axis=1)
    w_and_x_t = np.concatenate([a["L0_tok_W_lin"].T.reshape(FC, P, D).transpose(1, 0, 2), cols[:, :, 0:P]], axis=2)
    expert_w = a["L0_ffn_expert_w"].reshape(QUARTERS, PER_QUARTER, DC, P, D).transpose(3, 0, 2, 1, 4)

    first_small, small = np.zeros((TABLE_ROWS, FIRST_SMALL), f32), np.zeros((P, SMALL), f32)
    bias_small = np.zeros((EB_ROWS, BIAS_SMALL), f32)
    packed = ((first_small, FIRST_COL), (small, COL), (bias_small, BIAS_COL))

    def put(name, block, row=0):
        block = block.reshape(block.shape[0], -1)
        to, at = next((x, y) for x, y in packed if name in y)
        to[row:row + block.shape[0], at[name][0]:at[name][1]] = block

    position = a["L0_tok_position_embeddings"][0]
    table = np.concatenate([a["cls_tok"][0], position, a["L0_tok_class_token"][0], a["L0_tok_b_lin"][None]])
    onehot = np.zeros((ADDED_ROWS, SEQ), f32)
    onehot[0:SEQ] = np.eye(SEQ)
    onehot[SEQ, 1] = 1
    onehot[SEQ + 1, 2:] = 1
    onehot = np.tile(onehot, (1, IMAGES))[:, 0:ONEHOT]
    for row in (0, TABLE_LO):
        put("table", table, row)
        put("onehot", onehot, row)
    put("ident", np.eye(P, dtype=f32))
    wqkv = np.stack([a["L0_attn_W" + m].T.reshape(DC, P, HEAD) for m in "qkv"])
    put("wqkv", wqkv.transpose(2, 1, 0, 3))
    put("biases", np.stack([a["L0_attn_b" + m] for m in "qkv"], axis=1))
    r = np.arange(GROUP)
    is_open = (r[:, None] // SEQ == r[None, :] // SEQ) & (r[:, None] >= r[None, :])
    put("mask", np.where(is_open, f32(0), f32(CLOSED)))
    put("wo", a["L0_attn_Wo"].T)
    put("bo", np.broadcast_to(a["L0_attn_bo"], (P, D)))
    put("gate_w", a["L0_ffn_gate_w"].reshape(DC, P, EXPERTS).transpose(1, 0, 2))
    put("gate_b", np.broadcast_to(a["L0_ffn_gate_b"], (P, EXPERTS)))
    for row in (0, 32, 64):
        put("expert_b", a["L0_ffn_expert_b"], row)

    arrays = {"x_t": x_t, "w_and_x_t": w_and_x_t, "first_small": first_small, "small": small, "bias_small": bias_small,
              "expert_w": expert_w.reshape(P, QUARTERS * DC, BANK)}
    arrays = {k: np.ascontiguousarray(x) for k, x in arrays.items()}
    nc = bacc.Bacc("TRN2", target_bir_lowering=False, num_devices=1)
    args = [nc.dram_tensor(k, x.shape, F32, kind="ExternalInput").ap() for k, x in arrays.items()]
    args.append(nc.dram_tensor("out", (TOKENS, D), F32, kind="ExternalOutput").ap())
    build(nc, *args)
    res = run_bass_kernel_spmd(nc, [arrays], core_ids=[0])
    return res.results[0]["out"].reshape(IMAGES, SEQ, D)
```
